# Optimizing a Trainium2 kernel written in Bass

```python
import numpy as np
import jax
import jax.numpy as jnp

def _softmax(x, axis=-1):
    return jax.nn.softmax(x, axis=axis)

def _gelu(x):
    return jax.nn.gelu(x, approximate=True)

def _silu(x):
    return jax.nn.silu(x)

def _sigmoid(x):
    return jax.nn.sigmoid(x)

def _layernorm(x, axis=-1, eps=1e-05):
    m = jnp.mean(x, axis=axis, keepdims=True)
    v = jnp.var(x, axis=axis, keepdims=True)
    return (x - m) / jnp.sqrt(v + eps)

def _scatter_add(tgt, idx, src, axis=0):
    return tgt.at[idx].add(src)

def _segment_sum(src, seg, n):
    return jax.ops.segment_sum(src, seg, n)
kernel_name = 'mk_seq_preln_d1_jaxref_r4_7d0c1f'

def setup_inputs(seed: int=0):
    np.random.seed(seed)
    _w = jnp.asarray

    def _L0_attn_setup():
        import jax, jax.numpy as jnp
        import numpy as np
        HEADS, DIM_HEAD, LANDMARKS, PINV_ITERS = (8, 64, 64, 6)
        WQK_DIM = 64
        CONV_K = 33

        def moore_penrose_pinv(x, iters):
            I = jnp.eye(x.shape[-1], dtype=x.dtype)
            abs_x = jnp.abs(x)
            scale = jnp.max(abs_x.sum(-1)) * jnp.max(abs_x.sum(-2))
            z = jnp.swapaxes(x, -1, -2) / scale
            for _ in range(iters):
                xz = x @ z
                z = 0.25 * z @ (13 * I - xz @ (15 * I - xz @ (7 * I - xz)))
            return z

        def nystrom_attention(x, qkv_w, out_w, out_b, conv_w):
            b, n, d = x.shape
            h, dh, m = (HEADS, DIM_HEAD, LANDMARKS)
            scale = dh ** (-0.5)
            qkv = x @ qkv_w
            q, k, v = jnp.split(qkv, 3, axis=-1)
            split = lambda t: t.reshape(b, n, h, dh).transpose(0, 2, 1, 3)
            q, k, v = (split(q) * scale, split(k), split(v))
            l = n // m
            q_l = q.reshape(b, h, m, l, dh).mean(axis=3)
            k_l = k.reshape(b, h, m, l, dh).mean(axis=3)
            attn1 = jax.nn.softmax(jnp.einsum('bhid,bhjd->bhij', q, k_l), axis=-1)
            attn2 = jax.nn.softmax(jnp.einsum('bhid,bhjd->bhij', q_l, k_l), axis=-1)
            attn3 = jax.nn.softmax(jnp.einsum('bhid,bhjd->bhij', q_l, k), axis=-1)
            attn2_inv = moore_penrose_pinv(attn2, PINV_ITERS)
            out = attn1 @ (attn2_inv @ (attn3 @ v))
            pad = CONV_K // 2
            res = jax.lax.conv_general_dilated(v, conv_w, window_strides=(1, 1), padding=((pad, pad), (0, 0)), dimension_numbers=('NCHW', 'OIHW', 'NCHW'), feature_group_count=h)
            out = out + res
            out = out.transpose(0, 2, 1, 3).reshape(b, n, h * dh)
            return out @ out_w + out_b

        def _reference_tuple_inner(dense, adj_rows, adj_cols, adj_vals, wq, wk, wv_w, wv_b, qkv_w, out_w, out_b, conv_w):
            b, n, d = dense.shape
            xg = nystrom_attention(dense, qkv_w, out_w, out_b, conv_w)
            enc = xg[0] + dense
            q = enc @ wq
            k = enc @ wk
            scores = jnp.einsum('bid,bjd->bij', q, k) / jnp.sqrt(jnp.float32(WQK_DIM))
            data = scores[0]
            contrib = adj_vals * data[adj_rows, adj_cols]
            A_raw = jax.ops.segment_sum(contrib, adj_rows, num_segments=n)
            alpha = jax.nn.softmax(A_raw)
            value = dense @ wv_w + wv_b
            xl = alpha[:, None] * value
            wei = jax.nn.sigmoid(-xl)
            sw = wei * wei
            xo = xl * 2 * sw + 2 * enc * (1 - sw)
            return (xo, A_raw)
        key = jax.random.key(seed)
        ks = jax.random.split(key, 12)
        n, d, E = (2048, 256, 32768)
        inner = HEADS * DIM_HEAD
        s = lambda fan: (1.0 / np.sqrt(fan)).astype(np.float32) if isinstance(fan, np.ndarray) else np.float32(1.0 / np.sqrt(fan))
        return {'dense': jax.random.normal(ks[0], (1, n, d), jnp.float32), 'adj_rows': jax.random.randint(ks[1], (E,), 0, n), 'adj_cols': jax.random.randint(ks[2], (E,), 0, n), 'adj_vals': jax.random.uniform(ks[3], (E,), jnp.float32), 'wq': jax.random.normal(ks[4], (d, WQK_DIM), jnp.float32) * s(d), 'wk': jax.random.normal(ks[5], (d, WQK_DIM), jnp.float32) * s(d), 'wv_w': jax.random.normal(ks[6], (d, d), jnp.float32) * s(d), 'wv_b': jnp.zeros((d,), jnp.float32), 'qkv_w': jax.random.normal(ks[7], (d, 3 * inner), jnp.float32) * s(d), 'out_w': jax.random.normal(ks[8], (inner, d), jnp.float32) * s(inner), 'out_b': jnp.zeros((d,), jnp.float32), 'conv_w': jax.random.normal(ks[9], (HEADS, 1, CONV_K, 1), jnp.float32) * s(CONV_K)}
    _L0_attn_in = _L0_attn_setup()

    def _L0_ffn_setup():
        import jax, jax.numpy as jnp
        import numpy as np
        NUM_EXPERTS = 8
        TOP_K = 2
        FIXED_IDX = 0
        D_MODEL = 256
        D_FF = 1024
        B, S = (4, 512)

        def _route(flat_x, Wr):
            logits = flat_x @ Wr.T
            probs = jax.nn.softmax(logits.astype(jnp.float32), axis=-1).astype(flat_x.dtype)
            fixed_probs = probs[:, FIXED_IDX:FIXED_IDX + 1]
            remaining = probs[:, 1:]
            other_probs, other_local = jax.lax.top_k(remaining, TOP_K - 1)
            other_idx = other_local + 1
            topk_idx = jnp.concatenate([jnp.full((flat_x.shape[0], 1), FIXED_IDX, dtype=jnp.int32), other_idx], axis=1)
            topk_probs = jnp.concatenate([fixed_probs, other_probs], axis=1)
            topk_probs = topk_probs / jnp.clip(topk_probs.sum(axis=-1, keepdims=True), 1e-09)
            gates = jnp.sum(jax.nn.one_hot(topk_idx, NUM_EXPERTS, dtype=topk_probs.dtype) * topk_probs[..., None], axis=1)
            return gates
        key = jax.random.key(seed)
        ks = jax.random.split(key, 5)
        scale_r = 1.0 / np.sqrt(D_MODEL)
        return {'x': jax.random.normal(ks[0], (B, S, D_MODEL), dtype=jnp.float32), 'Wr': jax.random.normal(ks[1], (NUM_EXPERTS, D_MODEL), dtype=jnp.float32) * scale_r, 'W1': jax.random.normal(ks[2], (NUM_EXPERTS, D_FF, D_MODEL), dtype=jnp.float32) * scale_r, 'W2': jax.random.normal(ks[3], (NUM_EXPERTS, D_MODEL, D_FF), dtype=jnp.float32) * (1.0 / np.sqrt(D_FF)), 'W3': jax.random.normal(ks[4], (NUM_EXPERTS, D_FF, D_MODEL), dtype=jnp.float32) * scale_r}
    _L0_ffn_in = _L0_ffn_setup()
    _d = {'L0_attn_dense': _L0_attn_in['dense'], 'L0_attn_adj_rows': _L0_attn_in['adj_rows'], 'L0_attn_adj_cols': _L0_attn_in['adj_cols'], 'L0_attn_adj_vals': _L0_attn_in['adj_vals'], 'L0_attn_wq': _L0_attn_in['wq'], 'L0_attn_wk': _L0_attn_in['wk'], 'L0_attn_wv_w': _L0_attn_in['wv_w'], 'L0_attn_wv_b': _L0_attn_in['wv_b'], 'L0_attn_qkv_w': _L0_attn_in['qkv_w'], 'L0_attn_out_w': _L0_attn_in['out_w'], 'L0_attn_out_b': _L0_attn_in['out_b'], 'L0_attn_conv_w': _L0_attn_in['conv_w'], 'L0_ffn_Wr': _L0_ffn_in['Wr'], 'L0_ffn_W1': _L0_ffn_in['W1'], 'L0_ffn_W2': _L0_ffn_in['W2'], 'L0_ffn_W3': _L0_ffn_in['W3']}
    _x0 = _d['L0_attn_dense']
    _d['L0_attn_dense'] = jax.random.normal(jax.random.fold_in(jax.random.key(seed), 1), (4, 1024, 256), dtype=_x0.dtype)
    del _x0
    return _d

def reference(L0_attn_dense, L0_attn_adj_rows, L0_attn_adj_cols, L0_attn_adj_vals, L0_attn_wq, L0_attn_wk, L0_attn_wv_w, L0_attn_wv_b, L0_attn_qkv_w, L0_attn_out_w, L0_attn_out_b, L0_attn_conv_w, L0_ffn_Wr, L0_ffn_W1, L0_ffn_W2, L0_ffn_W3):

    def _L0_attn_ref(dense, adj_rows, adj_cols, adj_vals, wq, wk, wv_w, wv_b, qkv_w, out_w, out_b, conv_w):
        import jax, jax.numpy as jnp
        import numpy as np
        HEADS, DIM_HEAD, LANDMARKS, PINV_ITERS = (8, 64, 64, 6)
        WQK_DIM = 64
        CONV_K = 33

        def moore_penrose_pinv(x, iters):
            I = jnp.eye(x.shape[-1], dtype=x.dtype)
            abs_x = jnp.abs(x)
            scale = jnp.max(abs_x.sum(-1)) * jnp.max(abs_x.sum(-2))
            z = jnp.swapaxes(x, -1, -2) / scale
            for _ in range(iters):
                xz = x @ z
                z = 0.25 * z @ (13 * I - xz @ (15 * I - xz @ (7 * I - xz)))
            return z

        def nystrom_attention(x, qkv_w, out_w, out_b, conv_w):
            b, n, d = x.shape
            h, dh, m = (HEADS, DIM_HEAD, LANDMARKS)
            scale = dh ** (-0.5)
            qkv = x @ qkv_w
            q, k, v = jnp.split(qkv, 3, axis=-1)
            split = lambda t: t.reshape(b, n, h, dh).transpose(0, 2, 1, 3)
            q, k, v = (split(q) * scale, split(k), split(v))
            l = n // m
            q_l = q.reshape(b, h, m, l, dh).mean(axis=3)
            k_l = k.reshape(b, h, m, l, dh).mean(axis=3)
            attn1 = jax.nn.softmax(jnp.einsum('bhid,bhjd->bhij', q, k_l), axis=-1)
            attn2 = jax.nn.softmax(jnp.einsum('bhid,bhjd->bhij', q_l, k_l), axis=-1)
            attn3 = jax.nn.softmax(jnp.einsum('bhid,bhjd->bhij', q_l, k), axis=-1)
            attn2_inv = moore_penrose_pinv(attn2, PINV_ITERS)
            out = attn1 @ (attn2_inv @ (attn3 @ v))
            pad = CONV_K // 2
            res = jax.lax.conv_general_dilated(v, conv_w, window_strides=(1, 1), padding=((pad, pad), (0, 0)), dimension_numbers=('NCHW', 'OIHW', 'NCHW'), feature_group_count=h)
            out = out + res
            out = out.transpose(0, 2, 1, 3).reshape(b, n, h * dh)
            return out @ out_w + out_b

        def _reference_tuple_inner(dense, adj_rows, adj_cols, adj_vals, wq, wk, wv_w, wv_b, qkv_w, out_w, out_b, conv_w):
            b, n, d = dense.shape
            xg = nystrom_attention(dense, qkv_w, out_w, out_b, conv_w)
            enc = xg[0] + dense
            q = enc @ wq
            k = enc @ wk
            scores = jnp.einsum('bid,bjd->bij', q, k) / jnp.sqrt(jnp.float32(WQK_DIM))
            data = scores[0]
            contrib = adj_vals * data[adj_rows, adj_cols]
            A_raw = jax.ops.segment_sum(contrib, adj_rows, num_segments=n)
            alpha = jax.nn.softmax(A_raw)
            value = dense @ wv_w + wv_b
            xl = alpha[:, None] * value
            wei = jax.nn.sigmoid(-xl)
            sw = wei * wei
            xo = xl * 2 * sw + 2 * enc * (1 - sw)
            return (xo, A_raw)
        return _reference_tuple_inner(dense, adj_rows, adj_cols, adj_vals, wq, wk, wv_w, wv_b, qkv_w, out_w, out_b, conv_w)[0]

    def _L0_ffn_ref(x, Wr, W1, W2, W3):
        import jax, jax.numpy as jnp
        import numpy as np
        NUM_EXPERTS = 8
        TOP_K = 2
        FIXED_IDX = 0
        D_MODEL = 256
        D_FF = 1024
        B, S = (4, 512)

        def _route(flat_x, Wr):
            logits = flat_x @ Wr.T
            probs = jax.nn.softmax(logits.astype(jnp.float32), axis=-1).astype(flat_x.dtype)
            fixed_probs = probs[:, FIXED_IDX:FIXED_IDX + 1]
            remaining = probs[:, 1:]
            other_probs, other_local = jax.lax.top_k(remaining, TOP_K - 1)
            other_idx = other_local + 1
            topk_idx = jnp.concatenate([jnp.full((flat_x.shape[0], 1), FIXED_IDX, dtype=jnp.int32), other_idx], axis=1)
            topk_probs = jnp.concatenate([fixed_probs, other_probs], axis=1)
            topk_probs = topk_probs / jnp.clip(topk_probs.sum(axis=-1, keepdims=True), 1e-09)
            gates = jnp.sum(jax.nn.one_hot(topk_idx, NUM_EXPERTS, dtype=topk_probs.dtype) * topk_probs[..., None], axis=1)
            return gates
        batch, seq, d_model = x.shape
        flat_x = x.reshape(batch * seq, d_model)
        gates = _route(flat_x, Wr)
        out = jnp.zeros_like(flat_x)
        for e in range(NUM_EXPERTS):
            h = jax.nn.silu(flat_x @ W1[e].T) * (flat_x @ W3[e].T)
            out = out + gates[:, e:e + 1] * (h @ W2[e].T)
        return out.reshape(batch, seq, d_model)
    x = L0_attn_dense
    x = x + _L0_attn_ref(_layernorm(x, axis=-1), L0_attn_adj_rows, L0_attn_adj_cols, L0_attn_adj_vals, L0_attn_wq, L0_attn_wk, L0_attn_wv_w, L0_attn_wv_b, L0_attn_qkv_w, L0_attn_out_w, L0_attn_out_b, L0_attn_conv_w)
    x = x + _L0_ffn_ref(_layernorm(x, axis=-1), L0_ffn_Wr, L0_ffn_W1, L0_ffn_W2, L0_ffn_W3)
    return x

_drawn_inputs = setup_inputs


def setup_inputs(seed=0):
    import zlib

    import numpy as np

    out = dict(_drawn_inputs(seed))
    spreads = {'L0_attn_wv_b': (0.0, 2.0), 'L0_attn_out_b': (0.0, 0.1)}
    factors = {'L0_attn_adj_vals': 5.854, 'L0_attn_wq': 7.445, 'L0_attn_wk': 8.0, 'L0_attn_wv_w': 8.0}
    for name, (base, spread) in spreads.items():
        noise = np.random.default_rng([zlib.crc32(name.encode()), seed]).standard_normal(out[name].shape)
        drawn = base * np.exp(spread * noise) if base else spread * noise
        out[name] = jnp.asarray(drawn.astype(out[name].dtype))
    for name, factor in factors.items():
        out[name] = (out[name] * factor).astype(out[name].dtype)
    return out
```

```python
import numpy as np
import concourse.bass as bass
from concourse import mybir
from contextlib import ExitStack

F32 = mybir.dt.float32
F32R = mybir.dt.float32r
I32 = mybir.dt.int32
ACT = mybir.ActivationFunctionType
ALU = mybir.AluOpType
AX = mybir.AxisListType

P = 128
B, N, D = 4, 1024, 256
TOK = B * N
NT = TOK // P
NT0 = N // P
KD = D // P
H, DH, LM = 8, 64, 64
HP = H // 2
PER_LM = N // LM
ITERS = 6
TAPS = 33
PAD = TAPS // 2
WIN = P - 2 * PAD
NWIN = -(-N // WIN)
XT0W = (NWIN - 1) * WIN + P
EDGES = 32768
EC = EDGES // P
EPS = 1e-5
E_, FF = 8, 1024
NCH = FF // P
TS = 256
NRT = (TOK + (E_ - 1) * (TS - 1)) // TS
SLOTS = NRT * TS


class Mine:

    def __init__(self, engine, semaphore):
        self.engine, self.semaphore, self.n = engine, semaphore, 0

    def did(self, instruction):
        self.n += 1
        return instruction.then_inc(self.semaphore, 1)

    def settle(self):
        self.engine.wait_ge(self.semaphore, self.n)

    def step(self, instruction):
        self.did(instruction)
        self.settle()


def bcast(ap, shape):
    return ap.to_broadcast(shape)


def attention(nc, t, dense, w):
    X, XN, VAL, XT0, XG, PS = t["X"], t["XN"], t["VAL"], t["XT0"], t["XG"], t["PS"]
    IDENT = t["IDENT"]
    held = []
    with ExitStack() as ctx:
        def sb(name, shape, dt=F32):
            return ctx.enter_context(nc.sbuf_tensor(name, shape, dt))

        def sem(name):
            held.append(nc.alloc_semaphore(name))
            return held[-1]

        WQK = sb("WQK", [P, KD, 2 * H * DH])
        WQT = sb("WQT", [P, HP, D])
        WKT = sb("WKT", [P, HP, D])
        WV = sb("WV", [P, KD, H * DH])
        WO = sb("WO", [P, HP, D])
        OB = sb("OB", [P, D])
        BAND = sb("BAND", [P, H, WIN])
        HALF1 = sb("HALF1", [P, P])
        EYE = sb("EYE", [P, LM])
        ST = sb("ST", [P, NT, 6])
        MV = sb("MV", [P, NT, 2])
        STD = sb("STD", [P, NT])
        RSTD = sb("RSTD", [P, NT])
        XLT = sb("XLT", [P, KD, B * LM])
        QL = sb("QL", [P, HP, B * LM])
        KL = sb("KL", [P, HP, B * LM])
        MQ = sb("MQ", [P, KD, H * LM])
        MK = sb("MK", [P, KD, H * LM])
        A2 = sb("A2", [P, B * HP, LM])
        R2 = sb("R2", [P, 3, B * HP])
        PAIRMX = sb("PAIRMX", [P, 2])
        ALLMX = sb("ALLMX", [P, 2])
        RSC = sb("RSC", [P, 2])
        A0T = sb("A0T", [P, HP, LM])
        Z = sb("Z", [P, HP, LM])
        ZT = sb("ZT", [P, HP, LM])
        XZT = sb("XZT", [P, HP, LM])
        POLY = sb("POLY", [P, HP, LM])
        P1 = sb("P1", [P, 3, H * LM])
        R1 = sb("R1", [P, 3, 3, H])
        P3 = sb("P3", [P, 2, N])
        R3 = sb("R3", [P, 3, HP])
        P3T = VAL[:, 0:NT // 2, :].rearrange("p t d -> p (t d)").rearrange("p (t n) -> p t n", t=NT0)
        AT = sb("AT", [P, HP, N])
        BT = KL[:].rearrange("p c n -> p (c n)").rearrange("p (k n) -> p k n", k=KD)
        VW = MK
        RT = VAL[:, NT // 2:NT, :].rearrange("p t d -> p (t d)").rearrange("p (c n) -> p c n", c=HP)
        DV = sb("DV", [P, HP, DH])
        ETS = sb("ETS", [P, HP, LM])
        G = QL

        x_in = [sem(f"x_in{g}") for g in range(8)]
        w_in = {k: sem("in_" + k) for k in ("wqk", "wqt", "wkt", "wv", "wo", "ob", "band")}
        ident_set, half_set, eye_set = sem("ident_set"), sem("half_set"), sem("eye_set")
        vchain, achain = sem("vchain"), sem("achain")
        var_ready, std_ready, rstd_ready = sem("var_ready"), sem("std_ready"), sem("rstd_ready")
        xn_v, xn_p = sem("xn_v"), sem("xn_p")
        tr_done, xt_ready, lm_ready, pad_set = sem("tr_done"), sem("xt_ready"), sem("lm_ready"), sem("pad_set")
        qk_done, ql_ready, kl_ready = sem("qk_done"), sem("ql_ready"), sem("kl_ready")
        s2_done, fold_done, fold_ready = sem("s2_done"), sem("fold_done"), sem("fold_ready")
        s2_shift, s2_exp, a2_ready = sem("s2_shift"), sem("s2_exp"), sem("a2_ready")
        colsum_done, pair_ready, allmax_ready = sem("colsum_done"), sem("pair_ready"), sem("allmax_ready")
        a0t_done, z0_ready = sem("a0t_done"), sem("z0_ready")
        pinv_done, pinv_v, pinv_a = sem("pinv_done"), sem("pinv_v"), sem("pinv_a")
        s1_done, s1_shift, s1_exp, p1_ready = sem("s1_done"), sem("s1_shift"), sem("s1_exp"), sem("p1_ready")
        s3_done, s3_max, s3_exp = sem("s3_done"), sem("s3_max"), sem("s3_exp")
        at_done, at_ready, pt_done, pt_ready = sem("at_done"), sem("at_ready"), sem("pt_done"), sem("pt_ready")
        bt_done, bt_ready = sem("bt_done"), sem("bt_ready")
        vw_done, vw_ready, cv_done, rt_ready = sem("vw_done"), sem("vw_ready"), sem("cv_done"), sem("rt_ready")
        r3_ready = sem("r3_ready")
        d_done, d_ready, e_done, e_ready, g_done, g_ready = (
            sem("d_done"), sem("d_ready"), sem("e_done"), sem("e_ready"), sem("g_done"), sem("g_ready"))
        o_done, xg_ready = sem("o_done"), sem("xg_ready")

        NSTEP = 4 * ITERS
        S1_AT = {s: s for s in range(NT0)}
        AT_AT = {s + 2: s for s in range(NT0)}
        S3_AT = {2 * c: c for c in range(HP)}
        PT_AT = {2 * c + 2 + h: (c, h) for c in range(HP) for h in range(2)}
        VW_AT = {11 + i: i for i in range(NWIN)}
        CV_AT = {12 + i: i for i in range(NWIN)}
        BT_AT = {16 + i: i for i in range(4)}
        bank = lambda b: PS[:, b, :]
        half = lambda h: slice(DH * (h % 2), DH * (h % 2) + DH)

        block = ctx.enter_context(nc.Block())

        @block.sync
        def _(sp):
            xv = dense.rearrange("(g a p) d -> g p a d", g=8, p=P)
            for g in range(8):
                sp.dma_start(X[:, 4 * g:4 * g + 4, :], xv[g]).then_inc(x_in[g], 16)
                if g == 3:
                    sp.dma_start(WQK[:], w["wqk"].rearrange("(k p) n -> p k n", p=P)).then_inc(w_in["wqk"], 16)
            sp.dma_start(WKT[:], w["wkt"].rearrange("(c p) n -> p c n", p=P)).then_inc(w_in["wkt"], 16)
            sp.dma_start(WQT[:], w["wqt"].rearrange("(c p) n -> p c n", p=P)).then_inc(w_in["wqt"], 16)
            sp.dma_start(WV[:], w["wv"].rearrange("(k p) n -> p k n", p=P)).then_inc(w_in["wv"], 16)
            padded = w["convp"]
            sp.dma_start(BAND[:], bass.AP(padded.tensor, 0, [[1, P], [padded.shape[1], H], [1, WIN]]))\
                .then_inc(w_in["band"], 16)
            sp.dma_start(WO[:], w["wo"].rearrange("(c p) n -> p c n", p=P)).then_inc(w_in["wo"], 16)
            sp.dma_start(OB[:], w["ob"].partition_broadcast(P)).then_inc(w_in["ob"], 16)

        @block.gpsimd
        def _(pool):
            pool.memset(IDENT[:], 0.0).then_inc(ident_set, 1)
            pool.memset(EYE[:], 0.0).then_inc(eye_set, 1)
            pool.memset(HALF1[:], 0.0).then_inc(half_set, 1)
            pool.wait_ge(ident_set, 1)
            pool.affine_select(out=IDENT[:], in_=IDENT[:], compare_op=ALU.not_equal, fill=1.0, base=0,
                               pattern=[[-1, P]], channel_multiplier=1).then_inc(ident_set, 1)
            pool.memset(XT0[:, :, 0:PAD], 0.0).then_inc(pad_set, 1)
            pool.memset(XT0[:, :, PAD + N:XT0W], 0.0).then_inc(pad_set, 1)
            for h in range(2):
                pool.wait_ge(eye_set, 1 + h)
                pool.affine_select(out=EYE[:], in_=EYE[:], compare_op=ALU.not_equal, fill=1.0, base=-LM * h,
                                   pattern=[[-1, LM]], channel_multiplier=1).then_inc(eye_set, 1)
            pool.wait_ge(eye_set, 3)
            for h in range(2):
                pool.wait_ge(half_set, 1 + h)
                pool.memset(HALF1[DH * h:DH * h + DH, DH * h:DH * h + DH], 1.0).then_inc(half_set, 1)
            pool.wait_ge(half_set, 3)
            for g in range(2, 8):
                pool.wait_ge(rstd_ready, g + 1)
                for i in range(4 * g, 4 * g + 4):
                    pool.tensor_scalar(XN[:, i, :], X[:, i, :], MV[:, i, 0:1], RSTD[:, i:i + 1],
                                       ALU.subtract, ALU.mult).then_inc(xn_p, 1)
            pool.wait_ge(pair_ready, 2)
            pool.partition_all_reduce(ALLMX[:], PAIRMX[:], P, bass.bass_isa.ReduceOp.max).then_inc(allmax_ready, 1)

        @block.vector
        def _(dve):
            mine = Mine(dve, vchain)

            def stats(g):
                dve.wait_ge(x_in[g], 16)
                for i in range(4 * g, 4 * g + 4):
                    mine.did(dve.bn_stats(ST[:, i, :], X[:, i, :]))
                mine.settle()
                for i in range(4 * g, 4 * g + 4):
                    mine.did(dve.bn_aggr(MV[:, i, :], ST[:, i, :]))
                mine.settle()
                dve.tensor_scalar(STD[:, 4 * g:4 * g + 4], MV[:, 4 * g:4 * g + 4, 1], EPS, None, ALU.add)\
                    .then_inc(var_ready, 1)

            def rstd(g):
                dve.wait_ge(std_ready, g + 1)
                dve.reciprocal(RSTD[:, 4 * g:4 * g + 4], STD[:, 4 * g:4 * g + 4]).then_inc(rstd_ready, 1)

            def landmarks(q):
                if q < 4:
                    dve.wait_ge(xt_ready, q + 1)
                    src = XT0[:, :, PAD + 256 * q:PAD + 256 * q + 256]
                else:
                    dve.wait_ge(tr_done, q + 1)
                    src = bank(2 + q % 4).rearrange("p (k n) -> p k n", k=KD)
                dve.tensor_reduce(XLT[:, :, 16 * q:16 * q + 16], src.rearrange("p k (m l) -> p k m l", l=PER_LM),
                                  AX.X, ALU.add).then_inc(lm_ready, 1)

            for g in range(8):
                stats(g)
                rstd(g)
                if g < 2:
                    dve.wait_ge(rstd_ready, g + 1)
                    for i in range(4 * g, 4 * g + 4):
                        dve.tensor_scalar(XN[:, i, :], X[:, i, :], MV[:, i, 0:1], RSTD[:, i:i + 1],
                                          ALU.subtract, ALU.mult).then_inc(xn_v, 1)
                if g >= 2:
                    landmarks(2 * g - 4)
                    landmarks(2 * g - 3)
            for q in range(12, 16):
                landmarks(q)
            for c in range(HP):
                dve.wait_ge(qk_done, c + 1)
                dve.tensor_scalar(QL[:, c, :], bank((0, 1, 6, 7)[c])[:, 0:B * LM], 1.0 / (PER_LM * DH ** 0.5),
                                  None, ALU.mult).then_inc(ql_ready, 1)
            dve.wait_ge(s2_done, 1)
            s2 = PS[:, 2:4, :].rearrange("p b (m j) -> p (b m) j", j=LM)
            mine.step(dve.tensor_reduce(R2[:, 0, :], s2, AX.X, ALU.max))
            dve.tensor_tensor(A2[:], s2, bcast(R2[:, 0, :].unsqueeze(2), [P, B * HP, LM]), ALU.subtract)\
                .then_inc(s2_shift, 1)
            dve.wait_ge(s2_exp, 1)
            mine.step(dve.tensor_reduce(R2[:, 1, :], A2[:], AX.X, ALU.add))
            mine.step(dve.reciprocal(R2[:, 2, :], R2[:, 1, :]))
            dve.tensor_tensor(A2[:], A2[:], bcast(R2[:, 2, :].unsqueeze(2), [P, B * HP, LM]), ALU.mult)\
                .then_inc(a2_ready, 1)
            dve.wait_ge(a2_ready, 1)
            mine.step(dve.tensor_reduce(R2[:, 0, :], A2[:], AX.X, ALU.add))
            dve.tensor_reduce(PAIRMX[:, 0:1], R2[:, 0, :], AX.X, ALU.max).then_inc(pair_ready, 1)
            dve.wait_ge(colsum_done, 1)
            dve.tensor_reduce(PAIRMX[:, 1:2], PS[:, 6:8, :].rearrange("p b n -> p (b n)"), AX.X, ALU.max)\
                .then_inc(pair_ready, 1)
            dve.wait_ge(a0t_done, 1)
            mine.did(dve.tensor_copy(A0T[:], bank(0)[:, 0:HP * LM].rearrange("p (c j) -> p c j", j=LM)))
            dve.wait_ge(allmax_ready, 1)
            mine.step(dve.tensor_tensor(RSC[:, 0:1], ALLMX[:, 0:1], ALLMX[:, 1:2], ALU.mult))
            mine.step(dve.reciprocal(RSC[:, 1:2], RSC[:, 0:1]))
            dve.tensor_scalar(Z[:], A0T[:], RSC[:, 1:2], None, ALU.mult).then_inc(z0_ready, 1)
            dve.tensor_scalar(ZT[:], A2[:, 0:HP, :], RSC[:, 1:2], None, ALU.mult).then_inc(z0_ready, 1)

            def shift1(i):
                dve.wait_ge(s1_done, i + 1)
                if i >= 3:
                    dve.wait_ge(at_done, i - 2)
                s1 = bank(2 + i % 2).rearrange("p (h j) -> p h j", j=LM)
                mine.step(dve.tensor_reduce(R1[:, i % 3, 0, :], s1, AX.X, ALU.max))
                dve.tensor_tensor(P1[:, i % 3, :].rearrange("p (h j) -> p h j", j=LM), s1,
                                  bcast(R1[:, i % 3, 0, :].unsqueeze(2), [P, H, LM]), ALU.subtract)\
                    .then_inc(s1_shift, 1)

            def norm1(i):
                dve.wait_ge(s1_exp, i + 1)
                p1 = P1[:, i % 3, :].rearrange("p (h j) -> p h j", j=LM)
                mine.step(dve.tensor_reduce(R1[:, i % 3, 1, :], p1, AX.X, ALU.add))
                mine.step(dve.reciprocal(R1[:, i % 3, 2, :], R1[:, i % 3, 1, :]))
                dve.tensor_tensor(p1, p1, bcast(R1[:, i % 3, 2, :].unsqueeze(2), [P, H, LM]), ALU.mult)\
                    .then_inc(p1_ready, 1)

            for s in range(NSTEP):
                ph, pv = s % 4, bank(int(s % 4 == 2))[:, 0:HP * LM].rearrange("p (c j) -> p c j", j=LM)
                dve.wait_ge(pinv_done, s + 1)
                if ph < 3:
                    dve.scalar_tensor_tensor(out=POLY[:], in0=bcast(EYE[:].unsqueeze(1), [P, HP, LM]),
                                             scalar=(7.0, 15.0, 13.0)[ph], in1=pv, op0=ALU.mult,
                                             op1=ALU.subtract).then_inc(pinv_v, 1)
                else:
                    dve.tensor_scalar(Z[:], pv, 0.25, None, ALU.mult).then_inc(pinv_v, 1)
                if s - 1 in S1_AT:
                    norm1(S1_AT[s - 1])
                if s in S1_AT:
                    shift1(S1_AT[s])
                if s in S3_AT:
                    c = S3_AT[s]
                    dve.wait_ge(s3_done, c + 1)
                    dve.tensor_reduce(R3[:, 0, c:c + 1], PS[:, 4:6, :].rearrange("p b n -> p (b n)"), AX.X,
                                      ALU.max, negate=True).then_inc(s3_max, 1)
                if s - 1 in VW_AT:
                    i = VW_AT[s - 1]
                    dve.wait_ge(vw_done, i + 1)
                    if i >= 2:
                        dve.wait_ge(cv_done, i - 1)
                    dve.tensor_copy(VW[:, i % 2, :], bank(2 + i % 2)).then_inc(vw_ready, 1)
            dve.wait_ge(s3_exp, HP)
            dve.reciprocal(R3[:, 2, :], R3[:, 1, :]).then_inc(r3_ready, 1)
            dve.wait_ge(d_done, 1)
            dve.wait_ge(r3_ready, 1)
            dve.tensor_tensor(DV[:], bank(0)[:, 0:HP * DH].rearrange("p (c j) -> p c j", j=DH),
                              bcast(R3[:, 2, :].unsqueeze(2), [P, HP, DH]), ALU.mult).then_inc(d_ready, 1)
            dve.wait_ge(e_done, 1)
            dve.tensor_copy(ETS[:], bank(1)[:, 0:HP * LM].rearrange("p (c j) -> p c j", j=LM)).then_inc(e_ready, 1)
            dve.wait_ge(g_done, 1)
            dve.tensor_copy(G[:].rearrange("p c d -> p (c d)"), PS[:, 2:4, :].rearrange("p b n -> p (b n)"))\
                .then_inc(g_ready, 1)
            dve.wait_ge(w_in["ob"], 16)
            for i in range(NT0):
                dve.wait_ge(o_done, i + 1)
                dve.tensor_tensor(XG[:, i, :], bank(4 + i % 4)[:, 0:D], OB[:], ALU.add).then_inc(xg_ready, 1)

        @block.scalar
        def _(act):
            act.wait_ge(pad_set, 2)
            sqrts = [0]

            def std(g):
                act.wait_ge(var_ready, g + 1)
                act.activation(STD[:, 4 * g:4 * g + 4], STD[:, 4 * g:4 * g + 4], ACT.Sqrt).then_inc(std_ready, 1)

            def xt_copy(q):
                act.wait_ge(tr_done, q + 1)
                src = bank(2 + q % 4).rearrange("p (k n) -> p k n", k=KD)
                act.activation(XT0[:, :, PAD + 256 * q:PAD + 256 * q + 256], src, ACT.Copy).then_inc(xt_ready, 1)

            for g in range(8):
                std(g)
                if 2 <= g < 4:
                    xt_copy(2 * g - 4)
                    xt_copy(2 * g - 3)
            for c in range(HP):
                act.wait_ge(ql_ready, c + 1)
                act.activation(KL[:, c, :], bank((0, 1, 6, 7)[c])[:, B * LM:2 * B * LM], ACT.Copy,
                               scale=1.0 / PER_LM).then_inc(kl_ready, 1)
            act.wait_ge(s2_shift, 1)
            act.activation(A2[:], A2[:], ACT.Exp).then_inc(s2_exp, 1)
            for i, dst in enumerate((MK, MQ)):
                act.wait_ge(fold_done, i + 1)
                for k in range(KD):
                    act.activation(dst[:, k, :].rearrange("p (c r j) -> p r c j", c=HP, r=2),
                                   PS[:, 4 + 2 * k:6 + 2 * k, 0:HP * LM].rearrange("p r (c j) -> p r c j", c=HP),
                                   ACT.Copy, scale=DH ** -0.5 if i else 1.0).then_inc(fold_ready, 1)
            for s in range(NSTEP):
                ph, pv = s % 4, bank(1)[:, 0:HP * LM].rearrange("p (c j) -> p c j", j=LM)
                if ph == 0:
                    act.wait_ge(pinv_done, s + 1)
                    act.activation(XZT[:], pv, ACT.Copy).then_inc(pinv_a, 1)
                if ph == 3:
                    act.wait_ge(pinv_done, s + 1)
                    act.activation(ZT[:], pv, ACT.Copy, scale=0.25).then_inc(pinv_a, 1)
                if s in S1_AT:
                    i = S1_AT[s]
                    act.wait_ge(s1_shift, i + 1)
                    act.activation(P1[:, i % 3, :], P1[:, i % 3, :], ACT.Exp).then_inc(s1_exp, 1)
                if s in S3_AT:
                    c = S3_AT[s]
                    act.wait_ge(s3_max, c + 1)
                    if c >= 2:
                        act.wait_ge(pt_done, 2 * (c - 1))
                    act.activation(P3[:, c % 2, :], PS[:, 4:6, :].rearrange("p b n -> p (b n)"), ACT.Exp,
                                   bias=R3[:, 0, c:c + 1], accum_out=R3[:, 1, c:c + 1]).then_inc(s3_exp, 1)
                if s in PT_AT:
                    c, h = PT_AT[s]
                    act.wait_ge(pt_done, 2 * c + h + 1)
                    act.activation(P3T[:, 4 * h:4 * h + 4, P * c:P * c + P],
                                   bank(6).rearrange("p (t n) -> p t n", n=P), ACT.Copy).then_inc(pt_ready, 1)
                if s in AT_AT:
                    i = AT_AT[s]
                    act.wait_ge(at_done, i + 1)
                    act.activation(AT[:, :, P * i:P * i + P], bank(7).rearrange("p (c n) -> p c n", n=P),
                                   ACT.Copy).then_inc(at_ready, 1)
                if s in CV_AT:
                    i = CV_AT[s]
                    act.wait_ge(cv_done, i + 1)
                    n = min(WIN, N - WIN * i)
                    act.activation(RT[:, :, WIN * i:WIN * i + n],
                                   bank(7)[:, 0:HP * WIN].rearrange("p (c n) -> p c n", n=WIN)[:, :, 0:n],
                                   ACT.Copy).then_inc(rt_ready, 1)
                if s - 1 in BT_AT and BT_AT[s - 1] == 3:
                    act.wait_ge(bt_done, 4)
                    act.activation(KL[:].rearrange("p c n -> p (c n)"),
                                   PS[:, 4:6, :].rearrange("p b n -> p (b n)"), ACT.Copy).then_inc(bt_ready, 1)

        @block.tensor
        def _(pe):
            mm = pe.matmul
            pe.wait_ge(ident_set, 2)
            for q in range(16):
                for i in (2 * q, 2 * q + 1):
                    if i < 8:
                        pe.wait_ge(xn_v, i + 1)
                    else:
                        pe.wait_ge(xn_p, i - 7)
                if q >= 4:
                    pe.wait_ge(xt_ready, min(q - 3, 4))
                    pe.wait_ge(lm_ready, q - 3)
                for k in range(KD):
                    for j in range(2):
                        last = pe.transpose(bank(2 + q % 4)[:, (2 * k + j) * P:(2 * k + j + 1) * P],
                                            XN[:, 2 * q + j, k * P:k * P + P], IDENT[:])
                last.then_inc(tr_done, 1)
            pe.wait_ge(lm_ready, 16)
            pe.wait_ge(w_in["wqk"], 16)
            for c in range(HP):
                for i in range(2):
                    for k in range(KD):
                        col = i * H * DH + c * P
                        last = mm(bank((0, 1, 6, 7)[c])[:, i * B * LM:(i + 1) * B * LM], WQK[:, k, col:col + P],
                                  XLT[:, k, :], start=(k == 0), stop=(k == KD - 1))
                last.then_inc(qk_done, 1)
            pe.wait_ge(xt_ready, 4)
            pe.wait_ge(ql_ready, HP)
            pe.wait_ge(kl_ready, HP)
            for b in range(B):
                for h in range(H):
                    c = h // 2
                    o = ((b % 2) * HP + c) * LM
                    last = mm(bank(2 + b // 2)[half(h), o:o + LM], QL[half(h), c, LM * b:LM * b + LM],
                              KL[half(h), c, LM * b:LM * b + LM], start=True, stop=True)
            last.then_inc(s2_done, 1)
            for i, (src, small, name) in enumerate(((WKT, QL, "wkt"), (WQT, KL, "wqt"))):
                pe.wait_ge(w_in[name], 16)
                if i:
                    pe.wait_ge(fold_ready, KD)
                for k in range(KD):
                    for h in range(H):
                        c = h // 2
                        last = mm(bank(4 + 2 * k + h % 2)[:, LM * c:LM * c + LM], src[half(h), c, k * P:k * P + P],
                                  small[half(h), c, 0:LM], start=True, stop=True)
                last.then_inc(fold_done, 1)
            pe.wait_ge(fold_ready, 2 * KD)
            pe.wait_ge(a2_ready, 1)
            pe.wait_ge(half_set, 3)
            for i in range(2):
                last = mm(bank(6 + i), HALF1[:],
                          A2[:, 8 * i:8 * i + 8, :].rearrange("p m j -> p (m j)"), start=True, stop=True)
            last.then_inc(colsum_done, 1)
            pe.wait_ge(eye_set, 3)
            for h in range(H):
                last = mm(bank(0)[half(h), (h // 2) * LM:(h // 2) * LM + LM], A2[half(h), h // 2, :],
                          EYE[half(h), :], start=True, stop=True)
            last.then_inc(a0t_done, 1)

            def products(b, pairs):
                for n, (left, right) in enumerate(pairs):
                    for h in range(H):
                        o = (h // 2) * LM
                        last = mm(bank(b + n)[half(h), o:o + LM], left[half(h), h // 2, :], right[half(h), h // 2, :],
                                  start=True, stop=True)
                return last

            pe.wait_ge(z0_ready, 2)
            for s in range(NSTEP):
                it, ph = divmod(s, 4)
                if s:
                    pe.wait_ge(pinv_v, s)
                if ph == 0:
                    if it:
                        pe.wait_ge(pinv_a, 2 * it)
                    last = products(0, [(A0T, Z), (Z, A0T)])
                elif ph < 3:
                    if ph == 1:
                        pe.wait_ge(pinv_a, 2 * it + 1)
                    last = products(ph - 1, [(XZT, POLY)])
                else:
                    last = products(0, [(ZT, POLY), (POLY, ZT)])
                last.then_inc(pinv_done, 1)
                if s in S3_AT:
                    c = S3_AT[s]
                    if c:
                        pe.wait_ge(s3_exp, c)
                    for n in range(2):
                        for k in range(KD):
                            last = mm(bank(4 + n), MK[:, k, P * c:P * c + P],
                                      XT0[:, k, PAD + 512 * n:PAD + 512 * n + 512], start=(k == 0), stop=(k == 1))
                    last.then_inc(s3_done, 1)
                if s in S1_AT:
                    i = S1_AT[s]
                    if i >= 2:
                        pe.wait_ge(s1_shift, i - 1)
                    for k in range(KD):
                        last = mm(bank(2 + i % 2), XT0[:, k, PAD + P * i:PAD + P * i + P], MQ[:, k, :],
                                  start=(k == 0), stop=(k == 1))
                    last.then_inc(s1_done, 1)
                if s in PT_AT:
                    c, h = PT_AT[s]
                    pe.wait_ge(s3_exp, c + 1)
                    if 2 * c + h:
                        pe.wait_ge(pt_ready, 2 * c + h)
                    for j in range(4):
                        n = 4 * h + j
                        last = pe.transpose(bank(6)[:, P * j:P * j + P], P3[:, c % 2, P * n:P * n + P], IDENT[:])
                    last.then_inc(pt_done, 1)
                if s in AT_AT:
                    i = AT_AT[s]
                    pe.wait_ge(p1_ready, i + 1)
                    if i:
                        pe.wait_ge(at_ready, i)
                    for c in range(HP):
                        last = pe.transpose(bank(7)[:, P * c:P * c + P], P1[:, i % 3, P * c:P * c + P], IDENT[:])
                    last.then_inc(at_done, 1)
                if s in CV_AT:
                    i = CV_AT[s]
                    pe.wait_ge(vw_ready, i + 1)
                    if i:
                        pe.wait_ge(rt_ready, i)
                    else:
                        pe.wait_ge(at_ready, NT0)
                        pe.wait_ge(w_in["band"], 16)
                    for h in range(H):
                        last = mm(bank(7)[half(h), (h // 2) * WIN:(h // 2) * WIN + WIN],
                                  VW[:, i % 2, DH * h:DH * h + DH], BAND[:, h, ::-1], start=True, stop=True)
                    last.then_inc(cv_done, 1)
                if s in VW_AT:
                    i = VW_AT[s]
                    if i >= 2:
                        pe.wait_ge(vw_ready, i - 1)
                    else:
                        pe.wait_ge(s1_shift, NT0)
                        pe.wait_ge(w_in["wv"], 16)
                    for k in range(KD):
                        last = mm(bank(2 + i % 2), XT0[:, k, WIN * i:WIN * i + P], WV[:, k, :],
                                  start=(k == 0), stop=(k == 1))
                    last.then_inc(vw_done, 1)
                if s in BT_AT:
                    q = BT_AT[s]
                    if q == 0:
                        pe.wait_ge(s3_exp, HP)
                        pe.wait_ge(pt_ready, 2 * HP)
                    for n in (2 * q, 2 * q + 1):
                        for k in range(KD):
                            last = mm(bank(4 + k), XN[:, n, k * P:k * P + P], P3T[:, n, :],
                                      start=(n == 0), stop=(n == NT0 - 1))
                    last.then_inc(bt_done, 1)
            pe.wait_ge(bt_ready, 1)
            pe.wait_ge(pinv_v, NSTEP)
            pe.wait_ge(pinv_a, 2 * ITERS)
            for h in range(H):
                for k in range(KD):
                    last = mm(bank(0)[half(h), (h // 2) * DH:(h // 2) * DH + DH], BT[:, k, LM * h:LM * h + LM],
                              WV[:, k, DH * h:DH * h + DH], start=(k == 0), stop=(k == 1))
            last.then_inc(d_done, 1)
            pe.wait_ge(d_ready, 1)
            products(1, [(DV, ZT)]).then_inc(e_done, 1)
            pe.wait_ge(e_ready, 1)
            pe.wait_ge(w_in["wo"], 16)
            pe.wait_ge(vw_ready, NWIN)
            for h in range(H):
                c = h // 2
                last = mm(bank(2 + c // 2)[half(h), (c % 2) * D:(c % 2) * D + D], ETS[half(h), c, :],
                          WO[half(h), c, :], start=True, stop=True)
            last.then_inc(g_done, 1)
            pe.wait_ge(rt_ready, NWIN)
            for i in range(NT0):
                if i >= 4:
                    pe.wait_ge(xg_ready, i - 3)
                for c in range(HP):
                    mm(bank(4 + i % 4)[:, 0:D], RT[:, c, P * i:P * i + P], WO[:, c, :], start=(c == 0), stop=False)
                if i == 0:
                    pe.wait_ge(g_ready, 1)
                for c in range(HP):
                    last = mm(bank(4 + i % 4)[:, 0:D], AT[:, c, P * i:P * i + P], G[:, c, :],
                              start=False, stop=(c == HP - 1))
                last.then_inc(o_done, 1)
    nc.clear_and_free_semaphores(held)
    nc.all_engine_barrier()


GC = 32
NG = EC // GC
R32 = 32


def adjacency(nc, t, rows, cols, vals, wq, wk, wvw, wvb, scores):
    X, XN, VAL, XT0, XG, PS = t["X"], t["XN"], t["VAL"], t["XT0"], t["XG"], t["PS"]
    IDENT, AL, NAL = t["IDENT"], t["AL"], t["NAL"]
    held = []
    with ExitStack() as ctx:
        def sb(name, shape, dt=F32):
            return ctx.enter_context(nc.sbuf_tensor(name, shape, dt))

        def sem(name):
            held.append(nc.alloc_semaphore(name))
            return held[-1]

        WQ = sb("WQ", [P, KD, DH])
        WK = sb("WK", [P, KD, DH])
        WVW = sb("WVW", [P, KD, D])
        WVB = sb("WVB", [P, D])
        ROWS = sb("ROWS", [P, EC], I32)
        COLS = sb("COLS", [P, EC], I32)
        VALS = sb("VALS", [P, EC])
        IDX = sb("IDX", [P, EC], I32)
        RHI = sb("RHI", [P, EC])
        RLO = sb("RLO", [P, EC])
        TMPI = sb("TMPI", [P, 2, EC], I32)
        IOTA = sb("IOTA", [P, R32])
        SEL = sb("SEL", [R32, 4, NT0])
        ZERO = sb("ZERO", [P, R32])
        STG = sb("STG", [P, 2, GC], I32)
        GOT = sb("GOT", [P, 2, GC])
        OHH = sb("OHH", [P, 2, GC, R32])
        OHL = sb("OHL", [P, 2, GC, R32])
        E0T = sb("E0T", [P, KD, N])
        QT = sb("QT", [DH, N])
        KT = sb("KT", [DH, N])
        SC = sb("SC", [P, 2, N])
        XTV = sb("XTV", [P, 2, KD, 2 * P])
        AS = sb("AS", [R32, R32])
        AP_ = sb("AP_", [P, NT0])
        RED = sb("RED", [P, 6])

        w_in = {k: sem("inb_" + k) for k in ("wq", "wk", "wvw", "wvb", "rows", "cols", "vals")}
        consts, sel_set = sem("consts"), sem("sel_set")
        vchain = sem("vchain_b")
        enc_ready, et_done, et_ready = sem("enc_ready"), sem("et_done"), sem("et_ready")
        q_done, q_ready, k_ready = sem("q_done"), sem("q_ready"), sem("k_ready")
        sc_done, sc_a, sc_v, sc_out = sem("sc_done"), sem("sc_a"), sem("sc_v"), [sem("sc_out0"), sem("sc_out1")]
        xt_done, xt_ready, val_done, val_ready = sem("xtv_done"), sem("xtv_ready"), sem("val_done"), sem("val_ready")
        idx_ready, staged, got = sem("idx_ready"), sem("staged"), [sem("got0"), sem("got1")]
        taken, oh_ready, oh_used, opened = sem("taken"), sem("oh_ready"), sem("oh_used"), sem("opened")
        a_done, as_ready, al_done, ap_ready = sem("a_done"), sem("as_ready"), sem("al_done"), sem("ap_ready")
        mx_ready, allmx, e_ready, allsum = sem("mx_ready"), sem("allmx"), sem("e_ready_b"), sem("allsum")
        neg_ready, xe_ready, going = sem("neg_ready"), sem("xe_ready"), sem("going")

        bank = lambda b: PS[:, b, :]
        block = ctx.enter_context(nc.Block())
        table = scores.rearrange("n (m o) -> (n m) o", o=1)

        @block.sync
        def _(sp):
            for dst, src, name in ((ROWS, rows, "rows"), (COLS, cols, "cols"), (VALS, vals, "vals")):
                sp.dma_start(dst[:], src.rearrange("(p j) -> p j", p=P)).then_inc(w_in[name], 16)
            for dst, src, name in ((WQ, wq, "wq"), (WK, wk, "wk"), (WVW, wvw, "wvw")):
                sp.dma_start(dst[:], src.rearrange("(k p) n -> p k n", p=P)).then_inc(w_in[name], 16)
            sp.dma_start(WVB[:], wvb.partition_broadcast(P)).then_inc(w_in["wvb"], 16)
            for i in range(NT0):
                sp.wait_ge(sc_a, i + 1)
                sp.wait_ge(sc_v, i + 1)
                sp.dma_start(scores[P * i:P * i + P, :], SC[:, i % 2, :]).then_inc(sc_out[i % 2], 16)

        @block.gpsimd
        def _(pool):
            pool.iota(IOTA[:], pattern=[[1, R32]], base=0, channel_multiplier=0,
                      allow_small_or_imprecise_dtypes=True).then_inc(consts, 1)
            pool.memset(ZERO[:], 0.0).then_inc(consts, 1)
            pool.memset(SEL[:], 0.0).then_inc(sel_set, 1)
            pool.wait_ge(sel_set, 1)
            pool.affine_select(out=SEL[:], in_=SEL[:], compare_op=ALU.not_equal, fill=1.0, base=0,
                               pattern=[[-1, 4], [-4, NT0]], channel_multiplier=1).then_inc(sel_set, 1)
            pool.wait_ge(sc_out[0], 16 * (NT0 // 2))
            pool.wait_ge(sc_out[1], 16 * (NT0 // 2))
            with pool.Fori(0, NG // 2) as i:
                for u in range(2):
                    pool.wait_ge(taken, 2 * i + (u + 1))
                    pool.wait_ge(idx_ready, 1)
                    pool.tensor_copy(STG[:, u, :], IDX[:, bass.ds((2 * i + u) * GC, GC)]).then_inc(staged, 1)
                    pool.wait_ge(staged, 2 * i + (u + 1))
                    pool.sem_inc(going, 1)
                    for j in range(GC):
                        pool.indirect_dma_start(GOT[:, u, j:j + 1], None, table,
                                                bass.IndirectOffsetOnAxis(ap=STG[:, u, j:j + 1], axis=0))\
                            .then_inc(got[u], 16)
            pool.wait_ge(mx_ready, 1)
            pool.partition_all_reduce(RED[:, 1:2], RED[:, 0:1], P, bass.bass_isa.ReduceOp.max).then_inc(allmx, 1)
            pool.wait_ge(e_ready, 1)
            pool.partition_all_reduce(RED[:, 4:5], RED[:, 3:4], P, bass.bass_isa.ReduceOp.add).then_inc(allsum, 1)

        @block.vector
        def _(dve):
            mine = Mine(dve, vchain)
            for q in range(4):
                dve.tensor_tensor(XN[:, 2 * q:2 * q + 2, :], XN[:, 2 * q:2 * q + 2, :], XG[:, 2 * q:2 * q + 2, :],
                                  ALU.add).then_inc(enc_ready, 1)
            dve.wait_ge(w_in["rows"], 16)
            dve.wait_ge(w_in["cols"], 16)
            mine.did(dve.tensor_scalar(TMPI[:, 0, :], ROWS[:], N - 1, None, ALU.min))
            mine.step(dve.tensor_scalar(TMPI[:, 1, :], COLS[:], N - 1, None, ALU.min))
            dve.scalar_tensor_tensor(out=IDX[:], in0=TMPI[:, 0, :], scalar=float(N), in1=TMPI[:, 1, :],
                                     op0=ALU.mult, op1=ALU.add).then_inc(idx_ready, 1)
            dve.wait_ge(idx_ready, 1)
            mine.did(dve.tensor_scalar(TMPI[:, 0, :], ROWS[:], 5, None, ALU.logical_shift_right))
            mine.step(dve.tensor_scalar(TMPI[:, 1, :], ROWS[:], R32 - 1, None, ALU.bitwise_and))
            mine.did(dve.tensor_copy(RHI[:], TMPI[:, 0, :]))
            mine.step(dve.tensor_copy(RLO[:], TMPI[:, 1, :]))
            dve.sem_inc(taken, 2)
            for n in range(2):
                dve.wait_ge(q_done, 2 * n + 2)
                dve.tensor_copy(KT[:, 512 * n:512 * n + 512], bank(3 + 2 * n)[0:DH, :]).then_inc(k_ready, 1)
            for i in range(NT0):
                dve.wait_ge(sc_done, i + 1)
                if i >= 2:
                    dve.wait_ge(sc_out[i % 2], 16 * (i // 2))
                dve.tensor_copy(SC[:, i % 2, 512:1024], bank(6 * (1 - i % 2) + 1)).then_inc(sc_v, 1)
            dve.wait_ge(w_in["wvb"], 16)
            for q in range(16):
                dve.wait_ge(val_done, q + 1)
                dve.tensor_tensor(VAL[:, 2 * q:2 * q + 2, :], bank(4 + q % 2).rearrange("p (t d) -> p t d", t=2),
                                  bcast(WVB[:].unsqueeze(1), [P, 2, D]), ALU.add).then_inc(val_ready, 1)
                if q >= 4:
                    dve.wait_ge(xt_done, q - 3)
                    dve.tensor_tensor(XN[:, 2 * q:2 * q + 2, :], XN[:, 2 * q:2 * q + 2, :],
                                      XG[:, 2 * (q % 4):2 * (q % 4) + 2, :], ALU.add).then_inc(enc_ready, 1)
            for q in range(4):
                if not q:
                    dve.wait_ge(enc_ready, 16)
                sl = slice(8 * q, 8 * q + 8)
                dve.scalar_tensor_tensor(out=X[:, sl, :], in0=XN[:, sl, :], scalar=2.0, in1=X[:, sl, :],
                                         op0=ALU.mult, op1=ALU.add).then_inc(xe_ready, 1)
            dve.wait_ge(consts, 2)
            dve.wait_ge(w_in["vals"], 16)
            for g in range(NG):
                u = g % 2
                cs = slice(GC * g, GC * g + GC)
                if g >= 2:
                    dve.wait_ge(oh_used, g - 1)
                three = [P, GC, R32]
                mine.did(dve.tensor_tensor(OHL[:, u], bcast(RLO[:, cs].unsqueeze(2), three),
                                           bcast(IOTA[:].unsqueeze(1), three), ALU.is_equal))
                mine.did(dve.tensor_tensor(OHH[:, u], bcast(RHI[:, cs].unsqueeze(2), three),
                                           bcast(IOTA[:].unsqueeze(1), three), ALU.is_equal))
                dve.wait_ge(got[u], 16 * GC * (g // 2 + 1))
                mine.step(dve.tensor_tensor(GOT[:, u, :], GOT[:, u, :], VALS[:, cs], ALU.mult))
                mine.step(dve.tensor_tensor(OHH[:, u], OHH[:, u], bcast(GOT[:, u, :].unsqueeze(2), three), ALU.mult))
                dve.sem_inc(taken, 1)
                dve.sem_inc(oh_ready, 1)
            dve.wait_ge(a_done, 1)
            dve.tensor_copy(AS[:], bank(0)[0:R32, 0:R32]).then_inc(as_ready, 1)
            dve.wait_ge(al_done, 1)
            mine.step(dve.tensor_copy(AP_[:], bank(1)[:, 0:NT0]))
            dve.tensor_reduce(RED[:, 0:1], AP_[:], AX.X, ALU.max).then_inc(mx_ready, 1)
            dve.wait_ge(allmx, 1)
            dve.tensor_scalar(RED[:, 2:3], RED[:, 1:2], -1.0, None, ALU.mult).then_inc(neg_ready, 1)
            dve.wait_ge(allsum, 1)
            mine.step(dve.reciprocal(RED[:, 5:6], RED[:, 4:5]))
            mine.step(dve.tensor_scalar(AL[:], AP_[:], RED[:, 5:6], None, ALU.mult))
            mine.step(dve.tensor_scalar(NAL[:], AL[:], -1.0, None, ALU.mult))

        @block.scalar
        def _(act):
            for q in range(4):
                act.wait_ge(et_done, q + 1)
                act.activation(E0T[:, :, 256 * q:256 * q + 256], bank(q % 2).rearrange("p (k n) -> p k n", k=KD),
                               ACT.Copy).then_inc(et_ready, 1)
                if q % 2:
                    n = q // 2
                    act.wait_ge(q_done, 2 * n + 1)
                    act.activation(QT[:, 512 * n:512 * n + 512], bank(2 + 2 * n)[0:DH, :], ACT.Copy,
                                   scale=DH ** -0.5).then_inc(q_ready, 1)
            for i in range(NT0):
                act.wait_ge(sc_done, i + 1)
                if i >= 2:
                    act.wait_ge(sc_out[i % 2], 16 * (i // 2))
                act.activation(SC[:, i % 2, 0:512], bank(6 * (1 - i % 2)), ACT.Copy).then_inc(sc_a, 1)
            for q in range(4, 16):
                act.wait_ge(xt_done, q - 3)
                if q >= 6:
                    act.wait_ge(val_done, q - 1)
                act.activation(XTV[:, q % 2], bank(2 + q % 2).rearrange("p (k n) -> p k n", k=KD), ACT.Copy)\
                    .then_inc(xt_ready, 1)
            act.wait_ge(neg_ready, 1)
            act.activation(AP_[:], AP_[:], ACT.Exp, bias=RED[:, 2:3], accum_out=RED[:, 3:4]).then_inc(e_ready, 1)

        @block.tensor
        def _(pe):
            mm = pe.matmul
            pe.wait_ge(w_in["wq"], 16)
            pe.wait_ge(w_in["wk"], 16)
            for q in range(4):
                pe.wait_ge(enc_ready, q + 1)
                if q >= 2:
                    pe.wait_ge(et_ready, q - 1)
                for k in range(KD):
                    for j in range(2):
                        last = pe.transpose(bank(q % 2)[:, (2 * k + j) * P:(2 * k + j + 1) * P],
                                            XN[:, 2 * q + j, k * P:k * P + P], IDENT[:])
                last.then_inc(et_done, 1)
                if q % 2:
                    n = q // 2
                    pe.wait_ge(et_ready, q + 1)
                    for i, wt in enumerate((WQ, WK)):
                        for k in range(KD):
                            last = mm(bank(2 + 2 * n + i)[0:DH, :], wt[:, k, :], E0T[:, k, 512 * n:512 * n + 512],
                                      start=(k == 0), stop=(k == 1))
                        last.then_inc(q_done, 1)
            pe.wait_ge(q_ready, 2)
            pe.wait_ge(k_ready, 2)
            for i in range(NT0):
                if i >= 2:
                    pe.wait_ge(sc_a, i - 1)
                    pe.wait_ge(sc_v, i - 1)
                for n in range(2):
                    last = mm(bank(6 * (1 - i % 2) + n), QT[:, P * i:P * i + P], KT[:, 512 * n:512 * n + 512],
                              start=True, stop=True)
                last.then_inc(sc_done, 1)
            pe.wait_ge(w_in["wvw"], 16)

            def values(q):
                if q >= 2:
                    pe.wait_ge(val_ready, q - 1)
                for j in range(2):
                    for k in range(KD):
                        if q < 4:
                            left = XT0[:, k, PAD + P * (2 * q + j):PAD + P * (2 * q + j) + P]
                        else:
                            left = XTV[:, q % 2, k, P * j:P * j + P]
                        last = mm(bank(4 + q % 2)[:, D * j:D * j + D], left, WVW[:, k, :], start=(k == 0), stop=(k == 1))
                last.then_inc(val_done, 1)

            for q in range(16):
                if q + 2 < 16 and q + 2 >= 4:
                    n = q + 2
                    if n >= 6:
                        pe.wait_ge(xt_ready, n - 5)
                    for k in range(KD):
                        for j in range(2):
                            last = pe.transpose(bank(2 + n % 2)[:, (2 * k + j) * P:(2 * k + j + 1) * P],
                                                XN[:, 2 * n + j, k * P:k * P + P], IDENT[:])
                    last.then_inc(xt_done, 1)
                if q >= 4:
                    pe.wait_ge(xt_ready, q - 3)
                values(q)
            pe.wait_ge(consts, 2)
            pe.wait_ge(sc_a, NT0)
            sums = bank(0)[0:R32, 0:R32]
            mm(sums, ZERO[:], ZERO[:], start=True, stop=False)
            with pe.Fori(0, NG // 2) as i:
                for u in range(2):
                    pe.wait_ge(oh_ready, 2 * i + (u + 1))
                    for j in range(GC):
                        last = mm(sums, OHH[:, u, j, :], OHL[:, u, j, :], start=False, stop=False)
                    last.then_inc(oh_used, 1)
            mm(sums, ZERO[:], ZERO[:], start=False, stop=True).then_inc(a_done, 1)
            pe.wait_ge(as_ready, 1)
            pe.wait_ge(sel_set, 2)
            for q in range(4):
                last = mm(bank(1)[R32 * q:R32 * q + R32, 0:NT0], AS[:], SEL[:, q, :], start=True, stop=True)
            last.then_inc(al_done, 1)
    nc.clear_and_free_semaphores(held)
    nc.all_engine_barrier()


NB = B
NGRP = NT // NB
SUB = TS // P
NSUB = NRT * SUB
ROUTED = E_ - 1


def group(ap, i):
    return ap[:].rearrange("p (b i) d -> p i b d", b=NB)[:, i]


def routing(nc, t, wrt, xh_rows, slots):
    X, XN, VAL, XHH, XHL, PS = t["X"], t["XN"], t["VAL"], t["XHH"], t["XHL"], t["PS"]
    IDENT, AL, NAL, G0, TEX = t["IDENT"], t["AL"], t["NAL"], t["G0"], t["TEX"]
    held = []
    with ExitStack() as ctx:
        def sb(name, shape, dt=F32):
            return ctx.enter_context(nc.sbuf_tensor(name, shape, dt))

        def sem(name):
            held.append(nc.alloc_semaphore(name))
            return held[-1]

        SG = sb("SG", [P, 2, NB * D])
        M = sb("M", [P, 2, NB * D])
        ST = sb("ST2", [P, NT, 6])
        MV = sb("MV2", [P, NT, 2])
        STD = sb("STD2", [P, NT])
        RSTD = sb("RSTD2", [P, NT])
        WR = sb("WR", [P, KD, E_])
        WRH = sb("WRH", [P, KD, E_], F32R)
        WRL = sb("WRL", [P, KD, E_], F32R)
        LG = sb("LG", [P, NT, E_])
        R = sb("RR", [P, 6, NT])
        OH = sb("OH", [P, NT, ROUTED])
        CAND = sb("CAND", [P, NT, ROUTED])
        CNT = sb("CNT", [P, ROUTED, NT])
        CUM = sb("CUM", [P, ROUTED, NT])
        END = sb("END", [P, 4, ROUTED + 1])
        MANY = sb("MANY", [P, ROUTED, TOK // TS])
        MI = sb("MI", [P, TOK // TS])
        TI = sb("TI", [1, NRT])
        TC = sb("TC", [1, NRT, ROUTED])
        TE = sb("TE", [1, NRT])
        RANK = sb("RANK", [P, ROUTED])
        ONES = sb("ONES", [P, P])
        TRI = sb("TRI", [P, P])
        SLOT = sb("SLOT", [P, NT])
        SI = sb("SI", [P, 4, NT], I32)
        META = sb("META", [P, NT, 2])
        INIT = sb("INIT", [P, NSUB, 2])

        wr_in, wr_split, sigm = sem("wr_in"), sem("wr_split"), sem("sigm")
        consts, tri_set = sem("consts_c"), sem("tri_set")
        vchain = sem("vchain_c")
        sig_ready, m_ready, x2_ready = sem("sig_ready"), sem("m_ready"), sem("x2_ready")
        var_ready, std_ready, xh_ready = sem("var_ready_c"), sem("std_ready_c"), sem("xh_ready")
        rows_out, init_out, put = sem("rows_out"), sem("init_out"), sem("put")
        tr_done, hi_ready, lo_ready = sem("tr_done_c"), sem("hi_ready"), sem("lo_ready")
        lg_done, lg_ready, mx_off, ex_ready = sem("lg_done"), sem("lg_ready"), sem("mx_off"), sem("ex_ready")
        oh_ready, pre_done, addr_ready, meta_set = sem("oh_ready_c"), sem("pre_done"), sem("addr_ready"), sem("meta_set")

        bank = lambda b: PS[:, b, :]
        block = ctx.enter_context(nc.Block())

        @block.sync
        def _(sp):
            sp.dma_start(WR[:], wrt.rearrange("(k p) n -> p k n", p=P)).then_inc(wr_in, 16)
            sp.wait_ge(meta_set, 3)
            sp.dma_start(slots.rearrange("(p s) o -> p (s o)", p=P), INIT[:].rearrange("p s o -> p (s o)"))\
                .then_inc(init_out, 16)
            xv = xh_rows.rearrange("(b i p) d -> i p b d", b=NB, p=P)
            for i in range(NGRP):
                sp.wait_ge(xh_ready, NB * (i + 1))
                sp.dma_start(xv[i], group(VAL, i)).then_inc(rows_out, 16)
            sp.wait_ge(rows_out, 16 * NGRP)

        @block.gpsimd
        def _(pool):
            pool.iota(META[:].bitcast(I32).rearrange("p (i b) o -> p i b o", b=NB)[:, :, :, 0],
                      pattern=[[P, NGRP], [N, NB]], base=0, channel_multiplier=1).then_inc(meta_set, 1)
            pool.memset(INIT[:, :, 1], 0.0).then_inc(meta_set, 1)
            pool.iota(INIT[:].bitcast(I32)[:, :, 0], pattern=[[0, NSUB]], base=TOK, channel_multiplier=0)\
                .then_inc(meta_set, 1)
            pool.memset(ONES[:], 1.0).then_inc(consts, 1)
            pool.iota(MI[:], pattern=[[TS, TOK // TS]], base=0, channel_multiplier=0,
                      allow_small_or_imprecise_dtypes=True).then_inc(consts, 1)
            pool.iota(TI[:], pattern=[[1, NRT]], base=0, channel_multiplier=0,
                      allow_small_or_imprecise_dtypes=True).then_inc(consts, 1)
            pool.iota(RANK[:], pattern=[[-1, ROUTED]], base=ROUTED + 1, channel_multiplier=0,
                      allow_small_or_imprecise_dtypes=True).then_inc(consts, 1)
            pool.memset(TRI[:], 1.0).then_inc(tri_set, 1)
            pool.wait_ge(tri_set, 1)
            pool.affine_select(out=TRI[:], in_=TRI[:], compare_op=ALU.is_gt, fill=0.0, base=0,
                               pattern=[[1, P]], channel_multiplier=-1).then_inc(tri_set, 1)
            pool.wait_ge(init_out, 16)
            pool.wait_ge(addr_ready, 1)
            for i in range(NT):
                pool.indirect_dma_start(slots, bass.IndirectOffsetOnAxis(ap=SI[:, 3, i:i + 1], axis=0),
                                        META[:, i, :], None).then_inc(put, 16)
            pool.wait_ge(put, 16 * NT)

        @block.vector
        def _(dve):
            mine = Mine(dve, vchain)
            dve.wait_ge(wr_in, 16)
            mine.step(dve.tensor_copy(WRH[:], WR[:]))
            dve.tensor_tensor(WRL[:], WR[:], WRH[:].bitcast(F32), ALU.subtract).then_inc(wr_split, 1)
            for i in range(NGRP):
                m = M[:, i % 2, :]
                m4 = m.rearrange("p (b d) -> p b d", b=NB)
                mine.step(dve.scalar_tensor_tensor(out=m4, in0=group(VAL, i), scalar=AL[:, i:i + 1],
                                                   in1=group(XN, i), op0=ALU.mult, op1=ALU.subtract))
                dve.wait_ge(sig_ready, i + 1)
                dve.tensor_tensor(m, m, SG[:, i % 2, :], ALU.mult).then_inc(m_ready, 1)
                dve.wait_ge(m_ready, i + 1)
                mine.step(dve.scalar_tensor_tensor(out=group(X, i), in0=m4, scalar=2.0, in1=group(X, i),
                                                   op0=ALU.mult, op1=ALU.add))
                for b in range(NB):
                    mine.did(dve.bn_stats(ST[:, 8 * b + i, :], X[:, 8 * b + i, :]))
                mine.settle()
                for b in range(NB):
                    mine.did(dve.bn_aggr(MV[:, 8 * b + i, :], ST[:, 8 * b + i, :]))
            mine.settle()
            dve.tensor_scalar(STD[:], MV[:, :, 1], EPS, None, ALU.add).then_inc(var_ready, 1)
            dve.wait_ge(std_ready, 1)
            mine.step(dve.reciprocal(RSTD[:], STD[:]))

            def low(i):
                dve.wait_ge(hi_ready, i + 1)
                dve.tensor_tensor(XHL[:, i].rearrange("p k n -> p (k n)"),
                                  PS[:, 2 * (i % 2):2 * (i % 2) + 2, :].rearrange("p b n -> p (b n)"),
                                  XHH[:, i].bitcast(F32).rearrange("p k n -> p (k n)"), ALU.subtract)\
                    .then_inc(lo_ready, 1)

            for i in range(NGRP):
                for b in range(NB):
                    c = 8 * b + i
                    dve.tensor_scalar(VAL[:, c, :], X[:, c, :], MV[:, c, 0:1], RSTD[:, c:c + 1],
                                      ALU.subtract, ALU.mult).then_inc(xh_ready, 1)
                if i:
                    low(i - 1)
            low(NGRP - 1)
            dve.wait_ge(lg_ready, NGRP)
            full = [P, NT, E_]
            mine.step(dve.tensor_reduce(R[:, 0, :], LG[:], AX.X, ALU.max))
            dve.tensor_tensor(LG[:], LG[:], bcast(R[:, 0, :].unsqueeze(2), full), ALU.subtract).then_inc(mx_off, 1)
            dve.wait_ge(ex_ready, 1)
            mine.step(dve.tensor_reduce(R[:, 1, :], LG[:], AX.X, ALU.add))
            mine.step(dve.reciprocal(R[:, 2, :], R[:, 1, :]))
            mine.step(dve.tensor_tensor(LG[:], LG[:], bcast(R[:, 2, :].unsqueeze(2), full), ALU.mult))
            mine.step(dve.tensor_reduce(R[:, 3, :], LG[:, :, 1:E_], AX.X, ALU.max))
            mine.step(dve.tensor_tensor(R[:, 4, :], LG[:, :, 0], R[:, 3, :], ALU.add))
            mine.step(dve.tensor_scalar(R[:, 4, :], R[:, 4, :], 1e-9, None, ALU.max))
            mine.step(dve.reciprocal(R[:, 5, :], R[:, 4, :]))
            mine.did(dve.tensor_tensor(G0[:], LG[:, :, 0], R[:, 5, :], ALU.mult))
            dve.wait_ge(meta_set, 3)
            mine.did(dve.tensor_tensor(META[:, :, 1], R[:, 3, :], R[:, 5, :], ALU.mult))
            seven = [P, NT, ROUTED]
            mine.step(dve.tensor_tensor(CAND[:], LG[:, :, 1:E_], bcast(R[:, 3, :].unsqueeze(2), seven), ALU.is_equal))
            dve.wait_ge(consts, 4)
            mine.step(dve.tensor_tensor(CAND[:], CAND[:], bcast(RANK[:].unsqueeze(1), seven), ALU.mult))
            mine.step(dve.tensor_reduce(R[:, 0, :], CAND[:], AX.X, ALU.max))
            dve.tensor_tensor(OH[:], CAND[:], bcast(R[:, 0, :].unsqueeze(2), seven), ALU.is_equal).then_inc(oh_ready, 1)
            dve.wait_ge(pre_done, 1)
            mine.step(dve.tensor_copy(CNT[:], bank(7)[:, 0:NT * ROUTED].rearrange("p (t e) -> p e t", e=ROUTED)))
            mine.did(dve.memset(END[:], 0.0))
            mine.did(dve.memset(CAND[:], 1.0))
            mine.settle()
            flat = lambda a: a.rearrange("p e t -> p (e t)")
            mine.step(dve.tensor_tensor_scan(flat(CUM[:]), CAND[:].rearrange("p t e -> p (t e)"), flat(CNT[:]), 0.0,
                                             ALU.mult, ALU.add))
            mine.step(dve.tensor_copy(END[:, 0, 1:], CUM[:, :, NT - 1]))
            mine.step(dve.tensor_tensor(END[:, 1, 0:ROUTED], END[:, 0, 1:], END[:, 0, 0:ROUTED], ALU.subtract))
            many = [P, ROUTED, TOK // TS]
            mine.step(dve.tensor_tensor(MANY[:], bcast(END[:, 1, 0:ROUTED].unsqueeze(2), many),
                                        bcast(MI[:].unsqueeze(1), many), ALU.is_gt))
            mine.step(dve.tensor_reduce(END[:, 2, 0:ROUTED], MANY[:], AX.X, ALU.add))
            mine.step(dve.tensor_tensor_scan(END[:, 3, 0:ROUTED], CAND[:, 0, :], END[:, 2, 0:ROUTED], 0.0,
                                             ALU.mult, ALU.add))
            three = [1, NRT, ROUTED]
            mine.did(dve.tensor_tensor(TC[:], bcast(END[0:1, 3, 0:ROUTED].unsqueeze(1), three),
                                       bcast(TI[:].unsqueeze(2), three), ALU.is_le))
            mine.step(dve.tensor_tensor(END[:, 2, 0:ROUTED], END[:, 3, 0:ROUTED], END[:, 2, 0:ROUTED], ALU.subtract))
            mine.did(dve.tensor_reduce(TE[:], TC[:], AX.X, ALU.add))
            mine.step(dve.scalar_tensor_tensor(out=END[:, 2, 0:ROUTED], in0=END[:, 2, 0:ROUTED], scalar=float(TS),
                                               in1=END[:, 0, 0:ROUTED], op0=ALU.mult, op1=ALU.subtract))
            mine.did(dve.tensor_scalar(TEX[:], TE[:], ROUTED - 1.0, 1.0, ALU.min, ALU.add))
            mine.step(dve.tensor_tensor(CUM[:], CUM[:], CNT[:], ALU.subtract))
            mine.step(dve.tensor_tensor(CUM[:], CUM[:], bcast(END[:, 2, 0:ROUTED].unsqueeze(2), [P, ROUTED, NT]), ALU.add))
            mine.step(dve.tensor_tensor(CAND[:], bank(6)[:, 0:NT * ROUTED].rearrange("p (t e) -> p t e", e=ROUTED),
                                        CUM[:].rearrange("p e t -> p t e"), ALU.add))
            mine.step(dve.tensor_tensor(CAND[:], CAND[:], OH[:], ALU.mult))
            mine.step(dve.tensor_reduce(SLOT[:], CAND[:], AX.X, ALU.add))
            mine.step(dve.tensor_copy(SI[:, 0, :], SLOT[:]))
            mine.did(dve.tensor_scalar(SI[:, 1, :], SI[:, 0, :], TS.bit_length() - 1, SUB.bit_length() - 1,
                                       ALU.logical_shift_right, ALU.logical_shift_left))
            mine.did(dve.tensor_scalar(SI[:, 2, :], SI[:, 0, :], TS - 1, SUB.bit_length() - 1,
                                       ALU.bitwise_and, ALU.logical_shift_right))
            mine.step(dve.tensor_scalar(SI[:, 3, :], SI[:, 0, :], SUB - 1, None, ALU.bitwise_and))
            mine.step(dve.tensor_tensor(SI[:, 1, :], SI[:, 1, :], SI[:, 3, :], ALU.add))
            dve.scalar_tensor_tensor(out=SI[:, 3, :], in0=SI[:, 2, :], scalar=float(NSUB), in1=SI[:, 1, :],
                                     op0=ALU.mult, op1=ALU.add).then_inc(addr_ready, 1)

        @block.scalar
        def _(act):
            for i in range(NGRP):
                if i >= 2:
                    act.wait_ge(m_ready, i - 1)
                act.activation(SG[:, i % 2, :].rearrange("p (b d) -> p b d", b=NB), group(VAL, i), ACT.Sigmoid,
                               scale=NAL[:, i:i + 1]).then_inc(sigm, 1)
                act.wait_ge(sigm, i + 1)
                act.activation(SG[:, i % 2, :], SG[:, i % 2, :], ACT.Square).then_inc(sig_ready, 1)
            act.wait_ge(var_ready, 1)
            act.activation(STD[:], STD[:], ACT.Sqrt).then_inc(std_ready, 1)

            def logits(i):
                act.wait_ge(lg_done, i + 1)
                act.activation(LG[:, NB * i:NB * i + NB, :], bank(4 + i % 2)[:, 0:NB * E_]
                               .rearrange("p (b e) -> p b e", e=E_), ACT.Copy).then_inc(lg_ready, 1)

            for i in range(NGRP):
                act.wait_ge(tr_done, i + 1)
                act.activation(XHH[:, i].rearrange("p k n -> p (k n)"),
                               PS[:, 2 * (i % 2):2 * (i % 2) + 2, :].rearrange("p b n -> p (b n)"), ACT.Copy)\
                    .then_inc(hi_ready, 1)
                if i:
                    logits(i - 1)
            logits(NGRP - 1)
            act.wait_ge(mx_off, 1)
            act.activation(LG[:], LG[:], ACT.Exp).then_inc(ex_ready, 1)

        @block.tensor
        def _(pe):
            mm = pe.matmul
            pe.wait_ge(wr_split, 1)

            def logits(i):
                pe.wait_ge(lo_ready, i + 1)
                if i >= 2:
                    pe.wait_ge(lg_ready, i - 1)
                for b in range(NB):
                    n = 0
                    for left in (XHH, XHL):
                        for right in (WRH, WRL):
                            for k in range(KD):
                                last = mm(bank(4 + i % 2)[:, E_ * b:E_ * b + E_], left[:, i, k, P * b:P * b + P],
                                          right[:, k, :], start=(n == 0), stop=(n == 7))
                                n += 1
                last.then_inc(lg_done, 1)

            for i in range(NGRP):
                pe.wait_ge(xh_ready, NB * (i + 1))
                if i >= 2:
                    pe.wait_ge(lo_ready, i - 1)
                for k in range(KD):
                    for b in range(NB):
                        last = pe.transpose(bank(2 * (i % 2) + k)[:, P * b:P * b + P],
                                            VAL[:, 8 * b + i, k * P:k * P + P], IDENT[:])
                last.then_inc(tr_done, 1)
                if i:
                    logits(i - 1)
            logits(NGRP - 1)
            pe.wait_ge(oh_ready, 1)
            pe.wait_ge(tri_set, 2)
            pe.wait_ge(consts, 4)
            for b, left in ((6, TRI), (7, ONES)):
                last = mm(bank(b)[:, 0:NT * ROUTED], left[:], OH[:].rearrange("p t e -> p (t e)"),
                          start=True, stop=True)
            last.then_inc(pre_done, 1)
    nc.clear_and_free_semaphores(held)
    nc.all_engine_barrier()


CW = 2 * D + D
RING = 4
AHEAD = (2, 5)
AHEAD_LOW = (2, 4)
SH = NGRP * NCH


def experts(nc, t, wpack, xh_rows, acc, slots, out):
    X, XN, VAL, XHH, XHL, PS = t["X"], t["XN"], t["VAL"], t["XHH"], t["XHL"], t["PS"]
    IDENT, G0, TEX = t["IDENT"], t["G0"], t["TEX"]
    held = []
    with ExitStack() as ctx:
        def sb(name, shape, dt=F32):
            return ctx.enter_context(nc.sbuf_tensor(name, shape, dt))

        def sem(name):
            held.append(nc.alloc_semaphore(name))
            return held[-1]

        xn, val = XN[:].rearrange("p t d -> p (t d)"), VAL[:].rearrange("p t d -> p (t d)")
        WB = [xn[:, 0:NCH * CW], val[:, 0:NCH * CW]]
        left = NCH * CW
        HF = xn[:, left:left + 1024].rearrange("p (u n) -> p u n", u=2)
        OUTR = xn[:, left + 1024:left + 2048].rearrange("p (u s d) -> p u s d", u=2, s=SUB)
        XR = val[:, left:left + 1024].rearrange("p (u s d) -> p u s d", u=2, s=SUB)
        AC = val[:, left + 1024:left + 2048].rearrange("p (u s d) -> p u s d", u=2, s=SUB)
        WSH = sb("WSH", [P, RING, CW], F32R)
        WSL = sb("WSL", [P, RING, CW], F32R)
        HH = sb("HH", [P, RING, 512], F32R)
        HL = sb("HL", [P, RING, 512], F32R)
        XTH, XTL = (x[:, 0].rearrange("p k (u n) -> p u k n", u=2) for x in (XHH, XHL))
        ws_slots = [[W[:, i, :] for i in range(RING)] +
                    [x[:, 1 + i].rearrange("p k n -> p (k n)")[:, 0:CW] for i in range(RING)]
                    for W, x in ((WSH, XHH), (WSL, XHL))]
        ws = lambda part, c, routed: ws_slots[part][c if routed else c % RING]
        SGT = sb("SGT", [P, 2, 512])
        TB = sb("TB", [P, NSUB, 2])
        TG = sb("TG", [P, NSUB], I32)
        STC = sb("STC", [P, 2, SUB], I32)
        STR = sb("STR", [P, 2, SUB], I32)
        GT = sb("GT", [P, 2, SUB])

        raw_in = [sem("raw_in0"), sem("raw_in1")]
        wh_ready, wl_ready = sem("wh_ready"), sem("wl_ready")
        up_done, silu_ready, h_ready = sem("up_done"), sem("silu_ready"), sem("h_ready")
        hh_ready, hl_ready, down_done = sem("hh_ready"), sem("hl_ready"), sem("down_done")
        y_done, y_read, acc_out = sem("y_done"), sem("y_read"), sem("acc_out")
        tb_in, tg_ready, gt_ready = sem("tb_in"), sem("tg_ready"), sem("gt_ready")
        staged, going = sem("staged_d"), sem("going_d")
        x_got, a_got = [sem("x_got0"), sem("x_got1")], [sem("a_got0"), sem("a_got1")]
        o_put = [sem("o_put0"), sem("o_put1")]
        tr_done, xh_done, xl_done = sem("tr_done_d"), sem("xh_done"), sem("xl_done")

        bank = lambda b: PS[:, b, :]
        block = ctx.enter_context(nc.Block())

        @block.sync
        def _(sp):
            sp.dma_start(WB[0], wpack[0:P, :]).then_inc(raw_in[0], 16)
            sp.dma_start(TB[:].rearrange("p s o -> p (s o)"), slots.rearrange("(p s) o -> p (s o)", p=P))\
                .then_inc(tb_in, 16)

            def load(tile, slot, wait):
                if wait is not None:
                    sp.wait_ge(wh_ready, wait)
                    sp.wait_ge(wl_ready, wait)
                expert = sp.value_load(TEX[0:1, bass.ds(tile, 1)], min_val=1, max_val=E_ - 1)
                sp.dma_start(WB[slot], wpack[bass.ds(expert * P, P), :]).then_inc(raw_in[slot], 16)

            load(0, 1, None)
            av = acc.rearrange("(b i p) d -> i p b d", b=NB, p=P)
            for i in range(NGRP):
                sp.wait_ge(y_read, i + 2)
                sp.dma_start(av[i], group(X, i)).then_inc(acc_out, 16)
            with sp.Fori(0, NRT // 2 - 1) as i:
                load(2 * i + 1, 0, SH + 16 * i)
                load(2 * i + 2, 1, SH + 8 + 16 * i)
            load(NRT - 1, 0, SH + 8 * (NRT - 2))

        @block.gpsimd
        def _(pool):
            def ready(semaphore, value):
                pool.wait_ge(semaphore, value)
                pool.sem_inc(going, 1)

            def fetch(tile, u, k):
                if k:
                    ready(tr_done, tile)
                pool.tensor_copy(STC[:, u, :], TG[:, bass.ds(tile * SUB, SUB)]).then_inc(staged, 1)
                ready(staged, 2 * tile if k else 1)
                for s in range(SUB):
                    pool.indirect_dma_start(XR[:, u, s, :], None, xh_rows,
                                            bass.IndirectOffsetOnAxis(ap=STC[:, u, s:s + 1], axis=0))\
                        .then_inc(x_got[u], 16)

            def finish(tile, u, k, more=True, first=False):
                if more:
                    fetch(tile + 1, 1 - u, True)
                for s in range(SUB):
                    pool.indirect_dma_start(AC[:, u, s, :], None, acc,
                                            bass.IndirectOffsetOnAxis(ap=STC[:, u, s:s + 1], axis=0))\
                        .then_inc(a_got[u], 16)
                if not first:
                    ready(o_put[u], 32 * k)
                pool.tensor_copy(STR[:, u, :], TB[:].bitcast(I32)[:, bass.ds(tile * SUB, SUB), 0]).then_inc(staged, 1)
                ready(staged, 2 * tile + (3 if more else 2))
                ready(y_read, NGRP + 2 + tile)
                for s in range(SUB):
                    pool.indirect_dma_start(out, bass.IndirectOffsetOnAxis(ap=STR[:, u, s:s + 1], axis=0),
                                            OUTR[:, u, s, :], None, bounds_check=TOK - 1, oob_is_err=False)\
                        .then_inc(o_put[u], 16)

            pool.sem_inc(tr_done, 1)
            pool.wait_ge(tg_ready, 1)
            fetch(0, 0, False)
            pool.wait_ge(acc_out, 16 * NGRP)
            finish(0, 0, 0, first=True)
            finish(1, 1, 0, first=True)
            with pool.Fori(1, NRT // 2 - 1) as i:
                finish(2 * i, 0, i)
                finish(2 * i + 1, 1, i)
            finish(NRT - 2, 0, NRT // 2 - 1)
            finish(NRT - 1, 1, NRT // 2 - 1, more=False)
            for u in range(2):
                pool.wait_ge(o_put[u], 16 * NRT)

        @block.scalar
        def _(act):
            def split(n, c, slot, routed, raw=None, strict=False):
                if raw is not None:
                    act.wait_ge(raw_in[slot], raw)
                act.wait_ge(down_done, n + 1 if strict or not routed else n + (1 - RING))
                act.activation(ws(0, c, routed), WB[slot][:, CW * c:CW * c + CW], ACT.Copy).then_inc(wh_ready, 1)

            def tile(n0, width, slot, follows, routed=True, then_routed=True):
                ahead = AHEAD[routed]
                for c in range(NCH):
                    act.wait_ge(up_done, n0 + (c + 1))
                    act.wait_ge(h_ready, n0 + (c + 1))
                    act.activation(SGT[:, c % 2, 0:width], bank(2 * (c % 2))[:, 0:width], ACT.Silu)\
                        .then_inc(silu_ready, 1)
                    act.wait_ge(h_ready, n0 + (c + 3))
                    act.wait_ge(down_done, n0 + (c + 1))
                    act.activation(HH[:, c % RING, 0:width], HF[:, c % 2, 0:width], ACT.Copy).then_inc(hh_ready, 1)
                    if c + ahead < NCH:
                        split(n0 + (c + ahead), c + ahead, slot, routed)
                    elif follows:
                        split(n0 + (c + ahead), c + ahead - NCH, follows[0], then_routed,
                              follows[1] if c + ahead == NCH else None, strict=not routed)

            def rows(t_, u):
                act.wait_ge(tr_done, t_ + 2)
                act.wait_ge(up_done, SH + 8 * t_ - 8)
                act.activation(XTH[:, u], bank(6 + u).rearrange("p (k n) -> p k n", k=KD), ACT.Copy).then_inc(xh_done, 1)

            act.sem_inc(hh_ready, 2)
            for c in range(AHEAD[0]):
                split(c, c, 0, False, 16 if c == 0 else None)
            with act.Fori(0, NGRP - 1) as i:
                tile(8 * i, 512, 0, (0, 16), routed=False, then_routed=False)
            tile(SH - NCH, 512, 0, (1, 16), routed=False)
            rows(0, 0)
            for c in range(AHEAD[0], AHEAD[1]):
                split(SH + c, c, 1, True, strict=c < RING)
            with act.Fori(0, NRT // 2 - 1) as i:
                tile(SH + 16 * i, TS, 1, (0, 16 * i + 32))
                rows(2 * i + 1, 1)
                tile(SH + 8 + 16 * i, TS, 0, (1, 16 * i + 32))
                rows(2 * i + 2, 0)
            tile(SH + 8 * (NRT - 2), TS, 1, (0, 16 * (NRT // 2) + 16))
            rows(NRT - 1, 1)
            tile(SH + 8 * (NRT - 1), TS, 0, None)

        @block.vector
        def _(dve):
            def split(n, c, slot, routed):
                dve.wait_ge(wh_ready, n + 1)
                dve.tensor_tensor(ws(1, c, routed), WB[slot][:, CW * c:CW * c + CW],
                                  ws(0, c, routed).bitcast(F32), ALU.subtract).then_inc(wl_ready, 1)

            def tile(n0, width, slot, follows, routed=True, then_routed=True):
                ahead = AHEAD_LOW[routed]
                for c in range(NCH):
                    dve.wait_ge(silu_ready, n0 + (c + 1))
                    dve.wait_ge(hh_ready, n0 + (c + 1))
                    dve.tensor_tensor(HF[:, c % 2, 0:width], SGT[:, c % 2, 0:width],
                                      bank(2 * (c % 2) + 1)[:, 0:width], ALU.mult).then_inc(h_ready, 1)
                    dve.wait_ge(hh_ready, n0 + (c + 3))
                    dve.tensor_tensor(HL[:, c % RING, 0:width], HF[:, c % 2, 0:width],
                                      HH[:, c % RING, 0:width].bitcast(F32), ALU.subtract).then_inc(hl_ready, 1)
                    if c + ahead < NCH:
                        split(n0 + (c + ahead), c + ahead, slot, routed)
                    elif follows is not None:
                        split(n0 + (c + ahead), c + ahead - NCH, follows, then_routed)

            def shared_out(i):
                dve.wait_ge(y_done, i + 1)
                for b in range(NB):
                    xt = X[:, bass.ds(8 * b + i, 1), :].rearrange("p o d -> p (o d)")
                    last = dve.scalar_tensor_tensor(out=xt, in0=bank(4 + b // 2)[:, D * (b % 2):D * (b % 2) + D],
                                                    scalar=G0[:, bass.ds(NB * i + b, 1)], in1=xt,
                                                    op0=ALU.mult, op1=ALU.add)
                last.then_inc(y_read, 1)

            def rows(t_, u):
                dve.wait_ge(xh_done, t_ + 1)
                dve.tensor_tensor(XTL[:, u], bank(6 + u).rearrange("p (k n) -> p k n", k=KD),
                                  XTH[:, u].bitcast(F32), ALU.subtract)\
                    .then_inc(xl_done, 1)

            def routed_out(t_, u, k, first=False):
                if not first:
                    dve.wait_ge(o_put[u], 32 * k)
                dve.tensor_copy(GT[:, u, :], TB[:, bass.ds(SUB * t_, SUB), 1]).then_inc(gt_ready, 1)
                dve.wait_ge(gt_ready, t_ + 1)
                dve.wait_ge(a_got[u], 32 * k + 32)
                dve.wait_ge(y_done, NGRP + 1 + t_)
                for s in range(SUB):
                    last = dve.scalar_tensor_tensor(out=OUTR[:, u, s, :], in0=bank(4 + u)[:, D * s:D * s + D],
                                                    scalar=GT[:, u, s:s + 1], in1=AC[:, u, s, :],
                                                    op0=ALU.mult, op1=ALU.add)
                last.then_inc(y_read, 1)

            dve.sem_inc(h_ready, 2)
            dve.sem_inc(y_read, 1)
            dve.wait_ge(tb_in, 16)
            dve.tensor_scalar(TG[:], TB[:].bitcast(I32)[:, :, 0], TOK - 1, None, ALU.min).then_inc(tg_ready, 1)
            for c in range(AHEAD_LOW[0]):
                split(c, c, 0, False)
            with dve.Fori(0, NGRP - 1) as i:
                tile(8 * i, 512, 0, 0, routed=False, then_routed=False)
                shared_out(i)
            tile(SH - NCH, 512, 0, 1, routed=False)
            rows(0, 0)
            shared_out(NGRP - 1)
            for c in range(AHEAD_LOW[0], AHEAD_LOW[1]):
                split(SH + c, c, 1, True)

            def pair(i, first=False):
                tile(SH + 16 * i, TS, 1, 0)
                rows(2 * i + 1, 1)
                routed_out(2 * i, 0, i, first)
                tile(SH + 8 + 16 * i, TS, 0, 1)
                rows(2 * i + 2, 0)
                routed_out(2 * i + 1, 1, i, first)

            pair(0, first=True)
            with dve.Fori(1, NRT // 2 - 1) as i:
                pair(i)
            tile(SH + 8 * (NRT - 2), TS, 1, 0)
            rows(NRT - 1, 1)
            routed_out(NRT - 2, 0, NRT // 2 - 1)
            tile(SH + 8 * (NRT - 1), TS, 0, None)
            routed_out(NRT - 1, 1, NRT // 2 - 1)

        @block.tensor
        def _(pe):
            def mm(*a, **k):
                return pe.matmul(*a, skip_group_check=True, **k)

            def three(ps, left, right, start, stop):
                ops = [(lh, r) for (lh, ll), (rh, rl) in zip(left, right) for r in (rh, rl)]
                ops += [(ll, rh) for (lh, ll), (rh, rl) in zip(left, right)]
                for n, (l, r) in enumerate(ops):
                    last = mm(ps, l, r, start=start and n == 0, stop=stop and n == len(ops) - 1)
                return last

            def up(n, c, xs, width, routed):
                pe.wait_ge(wl_ready, n + 1)
                pe.wait_ge(h_ready, n + 1)
                for half_ in range(2):
                    o = D * half_
                    w_ = [tuple(ws(part, c, routed)[:, o + P * k:o + P * k + P] for part in range(2))
                          for k in range(KD)]
                    last = three(bank(2 * (c % 2) + half_)[:, 0:width], w_, xs, True, True)
                last.then_inc(up_done, 1)

            def down(n, c, y, subs, routed):
                pe.wait_ge(hl_ready, n + 1)
                for s in range(subs):
                    hs = [tuple(h[:, c % RING, P * s:P * s + P] for h in (HH, HL))]
                    w_ = [tuple(ws(part, c, routed)[:, 2 * D:3 * D] for part in range(2))]
                    last = three(bank(y + s // 2)[:, D * (s % 2):D * (s % 2) + D], hs, w_,
                                 c == 0 and s % 2 == 0, c == NCH - 1)
                last.then_inc(down_done, 1)
                return last

            def rows(t_, u, k):
                pe.wait_ge(x_got[u], 32 * k + 32)
                if not isinstance(t_, int) or t_ >= 2:
                    pe.wait_ge(xl_done, t_ - 1)
                for k_ in range(KD):
                    for s in range(SUB):
                        last = pe.transpose(bank(6 + u)[:, TS * k_ + P * s:TS * k_ + P * s + P],
                                            XR[:, u, s, P * k_:P * k_ + P], IDENT[:])
                last.then_inc(tr_done, 1)

            def tile(n0, xs, width, y, subs, read, nxt, routed=True):
                up(n0, 0, xs, width, routed)
                up(n0 + 1, 1, xs, width, routed)
                for c in range(NCH):
                    if c + 2 < NCH:
                        up(n0 + (c + 2), c + 2, xs, width, routed)
                    if c == 0:
                        pe.wait_ge(y_read, read)
                    last = down(n0 + c, c, y, subs, routed)
                    if c == 4 and nxt:
                        rows(*nxt)
                pe.wait_ge(down_done, n0 + (NCH + RING))
                pe.sem_inc(y_done, 1)

            pe.sem_inc(down_done, RING)
            shared_x = lambda i: [tuple(x[:, bass.ds(i, 1), k, :].rearrange("p o n -> p (o n)")
                                        for x in (XHH, XHL)) for k in range(KD)]
            routed_x = lambda u: [tuple(x[:, u, k, :] for x in (XTH, XTL)) for k in range(KD)]
            with pe.Fori(0, NGRP - 1) as i:
                tile(8 * i, shared_x(i), 512, 4, NB, i + 1, None, routed=False)
            tile(SH - NCH, shared_x(NGRP - 1), 512, 4, NB, NGRP, (0, 0, 0), routed=False)

            def routed(t_, u, nxt):
                pe.wait_ge(xl_done, t_ + 1)
                tile(SH + 8 * t_, routed_x(u), TS, 4 + u, SUB, NGRP + 1 + t_, nxt)

            routed(0, 0, (1, 1, 0))
            with pe.Fori(0, NRT // 2 - 1) as i:
                routed(2 * i + 1, 1, (2 * i + 2, 0, i + 1))
                routed(2 * i + 2, 0, (2 * i + 3, 1, i + 1))
            routed(NRT - 1, 1, None)
    nc.clear_and_free_semaphores(held)
    nc.all_engine_barrier()


def program(nc, dense, wqk, wqt, wkt, wv, wo, ob, convp, rows, cols, vals, wq, wk, wvw, wvb, wrt, wpack, out):
    scores = nc.dram_tensor("scores", (N, N), F32, kind="Internal").ap()
    xh_rows = nc.dram_tensor("xh_rows", (TOK, D), F32, kind="Internal").ap()
    acc = nc.dram_tensor("acc", (TOK, D), F32, kind="Internal").ap()
    slots = nc.dram_tensor("slots", (SLOTS, 2), F32, kind="Internal").ap()
    with ExitStack() as whole:
        def sb(name, shape, dt=F32, ctx=whole):
            return ctx.enter_context(nc.sbuf_tensor(name, shape, dt))

        t = {
            "X": sb("X", [P, NT, D]), "XN": sb("XN", [P, NT, D]), "VAL": sb("VAL", [P, NT, D]),
            "IDENT": sb("IDENT", [P, P]), "AL": sb("AL", [P, NT0]), "NAL": sb("NAL", [P, NT0]),
            "G0": sb("G0", [P, NT]), "TEX": sb("TEX", [1, NRT], I32),
            "PS": whole.enter_context(nc.psum_tensor("PS", [P, 8, 512], F32)),
        }
        with ExitStack() as first:
            t["XT0"] = sb("XT0", [P, KD, XT0W], ctx=first)
            t["XG"] = sb("XG", [P, NT0, D], ctx=first)
            attention(nc, t, dense, {"wqk": wqk, "wqt": wqt, "wkt": wkt, "wv": wv, "wo": wo, "ob": ob, "convp": convp})
            adjacency(nc, t, rows, cols, vals, wq, wk, wvw, wvb, scores)
        t["XHH"] = sb("XHH", [P, NGRP, KD, 512], F32R)
        t["XHL"] = sb("XHL", [P, NGRP, KD, 512], F32R)
        routing(nc, t, wrt, xh_rows, slots)
        experts(nc, t, wpack, xh_rows, acc, slots, out)


def kernel(**inputs):
    import concourse.bacc as bacc
    from concourse.bass_utils import run_bass_kernel_spmd as run

    a = {k.replace("L0_", ""): np.asarray(v) for k, v in inputs.items()}
    qkv = a["attn_qkv_w"]
    convp = np.zeros((H, 2 * P), np.float32)
    convp[:, WIN - 1:WIN - 1 + TAPS] = a["attn_conv_w"][:, 0, :, 0]
    up = [a[n].reshape(E_, NCH, P, KD, P).transpose(0, 4, 1, 3, 2) for n in ("ffn_W1", "ffn_W3")]
    dn = a["ffn_W2"].reshape(E_, D, NCH, P).transpose(0, 3, 2, 1)
    wpack = np.concatenate([u.reshape(E_, P, NCH, D) for u in up] + [dn], axis=3)
    arrays = {
        "dense": a["attn_dense"].reshape(TOK, D),
        "wqk": qkv[:, :2 * H * DH], "wqt": qkv[:, :H * DH].T, "wkt": qkv[:, H * DH:2 * H * DH].T,
        "wv": qkv[:, 2 * H * DH:], "wo": a["attn_out_w"], "ob": a["attn_out_b"], "convp": convp,
        "rows": a["attn_adj_rows"], "cols": a["attn_adj_cols"], "vals": a["attn_adj_vals"],
        "wq": a["attn_wq"], "wk": a["attn_wk"], "wvw": a["attn_wv_w"], "wvb": a["attn_wv_b"],
        "wrt": a["ffn_Wr"].T, "wpack": wpack.reshape(E_ * P, NCH * CW),
    }
    arrays = {"in_" + k: np.ascontiguousarray(v) for k, v in arrays.items()}
    nc = bacc.Bacc("TRN2", target_bir_lowering=False, num_devices=1)
    args = [nc.dram_tensor(k, v.shape, mybir.dt.from_np(v.dtype), kind="ExternalInput").ap()
            for k, v in arrays.items()]
    out = nc.dram_tensor("out", (TOK, D), F32, kind="ExternalOutput").ap()
    program(nc, *args, out)
    result = run(nc, [arrays], core_ids=[0])
    return result.results[0]["out"].reshape(B, N, D)
```
